# Optimizing a Trainium2 kernel written in Bass

```python
import numpy as np
import jax
import jax.numpy as jnp

def _softmax(x, axis=-1):
    return jax.nn.softmax(x, axis=axis)

def _gelu(x):
    return jax.nn.gelu(x, approximate=True)

def _silu(x):
    return jax.nn.silu(x)

def _sigmoid(x):
    return jax.nn.sigmoid(x)

def _layernorm(x, axis=-1, eps=1e-05):
    m = jnp.mean(x, axis=axis, keepdims=True)
    v = jnp.var(x, axis=axis, keepdims=True)
    return (x - m) / jnp.sqrt(v + eps)

def _scatter_add(tgt, idx, src, axis=0):
    return tgt.at[idx].add(src)

def _segment_sum(src, seg, n):
    return jax.ops.segment_sum(src, seg, n)
kernel_name = 'mk_rec_standalone_d1_rec_r8_3c8f42'

def setup_inputs(seed: int=0):
    np.random.seed(seed)
    _w = jnp.asarray

    def _rec_inputs():
        import jax
        import jax.numpy as jnp
        _rk = jax.random.key(seed)
        r_dense = -0.00338568 + 1.0005 * jax.random.normal(jax.random.fold_in(_rk, 1), (2048, 13), jnp.float32)
        r_sparse_idx = jnp.stack([jax.random.randint(jax.random.fold_in(jax.random.fold_in(_rk, 2), 0), (2048,), 2, 12500, jnp.int32), jax.random.randint(jax.random.fold_in(jax.random.fold_in(_rk, 2), 1), (2048,), 1, 99999, jnp.int32), jax.random.randint(jax.random.fold_in(jax.random.fold_in(_rk, 2), 2), (2048,), 0, 12500, jnp.int32), jax.random.randint(jax.random.fold_in(jax.random.fold_in(_rk, 2), 3), (2048,), 5, 12500, jnp.int32), jax.random.randint(jax.random.fold_in(jax.random.fold_in(_rk, 2), 4), (2048,), 20, 99993, jnp.int32), jax.random.randint(jax.random.fold_in(jax.random.fold_in(_rk, 2), 5), (2048,), 0, 99993, jnp.int32), jax.random.randint(jax.random.fold_in(jax.random.fold_in(_rk, 2), 6), (2048,), 2, 99999, jnp.int32), jax.random.randint(jax.random.fold_in(jax.random.fold_in(_rk, 2), 7), (2048,), 2, 99995, jnp.int32), jax.random.randint(jax.random.fold_in(jax.random.fold_in(_rk, 2), 8), (2048,), 0, 99999, jnp.int32), jax.random.randint(jax.random.fold_in(jax.random.fold_in(_rk, 2), 9), (2048,), 2, 99986, jnp.int32), jax.random.randint(jax.random.fold_in(jax.random.fold_in(_rk, 2), 10), (2048,), 4, 99999, jnp.int32), jax.random.randint(jax.random.fold_in(jax.random.fold_in(_rk, 2), 11), (2048,), 15, 99999, jnp.int32), jax.random.randint(jax.random.fold_in(jax.random.fold_in(_rk, 2), 12), (2048,), 0, 99989, jnp.int32), jax.random.randint(jax.random.fold_in(jax.random.fold_in(_rk, 2), 13), (2048,), 5, 99990, jnp.int32), jax.random.randint(jax.random.fold_in(jax.random.fold_in(_rk, 2), 14), (2048,), 2, 99996, jnp.int32), jax.random.randint(jax.random.fold_in(jax.random.fold_in(_rk, 2), 15), (2048,), 3, 99994, jnp.int32), jax.random.randint(jax.random.fold_in(jax.random.fold_in(_rk, 2), 16), (2048,), 0, 99998, jnp.int32), jax.random.randint(jax.random.fold_in(jax.random.fold_in(_rk, 2), 17), (2048,), 13, 99998, jnp.int32), jax.random.randint(jax.random.fold_in(jax.random.fold_in(_rk, 2), 18), (2048,), 10, 12498, jnp.int32), jax.random.randint(jax.random.fold_in(jax.random.fold_in(_rk, 2), 19), (2048,), 0, 99999, jnp.int32), jax.random.randint(jax.random.fold_in(jax.random.fold_in(_rk, 2), 20), (2048,), 0, 99995, jnp.int32), jax.random.randint(jax.random.fold_in(jax.random.fold_in(_rk, 2), 21), (2048,), 1, 99998, jnp.int32), jax.random.randint(jax.random.fold_in(jax.random.fold_in(_rk, 2), 22), (2048,), 1, 99997, jnp.int32), jax.random.randint(jax.random.fold_in(jax.random.fold_in(_rk, 2), 23), (2048,), 2, 99989, jnp.int32), jax.random.randint(jax.random.fold_in(jax.random.fold_in(_rk, 2), 24), (2048,), 6, 12500, jnp.int32), jax.random.randint(jax.random.fold_in(jax.random.fold_in(_rk, 2), 25), (2048,), 2, 99995, jnp.int32)], axis=1)
        return (r_dense, r_sparse_idx)
    r_dense, r_sparse_idx = _rec_inputs()

    def _L0_rec_setup():
        import jax, jax.numpy as jnp
        import numpy as np
        NUM_TABLES = 26
        VOCAB = 12500
        M_SPA = 64
        N_DENSE = 13
        LN_BOT = [512, 256, 64]
        LN_TOP = [512, 256, 1]
        BATCH = 2048

        def _dense_params(key, dims):
            Ws, bs = ([], [])
            for i in range(len(dims) - 1):
                key, k = jax.random.split(key)
                fan_in = dims[i]
                Ws.append(jax.random.normal(k, (dims[i], dims[i + 1]), jnp.float32) / np.sqrt(fan_in))
                bs.append(jnp.zeros((dims[i + 1],), jnp.float32))
            return (Ws, bs)
        key = jax.random.key(seed)
        k0, k1, k2, k3, k4 = jax.random.split(key, 5)
        dense = jax.random.normal(k0, (BATCH, N_DENSE), jnp.float32)
        sparse_idx = jax.random.randint(k1, (BATCH, NUM_TABLES), 0, VOCAB, jnp.int64)
        emb = jax.random.normal(k2, (NUM_TABLES, VOCAB, M_SPA), jnp.float32) * 0.01
        (Wb0, Wb1, Wb2), (bb0, bb1, bb2) = _dense_params(k3, [N_DENSE] + LN_BOT)
        n_inter = NUM_TABLES + 1
        top_in = M_SPA + n_inter * (n_inter - 1) // 2
        (Wt0, Wt1, Wt2), (bt0, bt1, bt2) = _dense_params(k4, [top_in] + LN_TOP)
        return dict(dense=dense, sparse_idx=sparse_idx, emb=emb, Wb0=Wb0, bb0=bb0, Wb1=Wb1, bb1=bb1, Wb2=Wb2, bb2=bb2, Wt0=Wt0, bt0=bt0, Wt1=Wt1, bt1=bt1, Wt2=Wt2, bt2=bt2)
    _L0_rec_all = _L0_rec_setup()
    _L0_rec_in = {k: v for k, v in _L0_rec_all.items() if k in ('emb', 'Wb0', 'bb0', 'Wb1', 'bb1', 'Wb2', 'bb2', 'Wt0', 'bt0', 'Wt1', 'bt1', 'Wt2', 'bt2')}
    del _L0_rec_all
    return {'r_dense': r_dense, 'r_sparse_idx': r_sparse_idx, 'L0_rec_emb': _L0_rec_in['emb'], 'L0_rec_Wb0': _L0_rec_in['Wb0'], 'L0_rec_bb0': _L0_rec_in['bb0'], 'L0_rec_Wb1': _L0_rec_in['Wb1'], 'L0_rec_bb1': _L0_rec_in['bb1'], 'L0_rec_Wb2': _L0_rec_in['Wb2'], 'L0_rec_bb2': _L0_rec_in['bb2'], 'L0_rec_Wt0': _L0_rec_in['Wt0'], 'L0_rec_bt0': _L0_rec_in['bt0'], 'L0_rec_Wt1': _L0_rec_in['Wt1'], 'L0_rec_bt1': _L0_rec_in['bt1'], 'L0_rec_Wt2': _L0_rec_in['Wt2'], 'L0_rec_bt2': _L0_rec_in['bt2']}

def reference(r_dense, r_sparse_idx, L0_rec_emb, L0_rec_Wb0, L0_rec_bb0, L0_rec_Wb1, L0_rec_bb1, L0_rec_Wb2, L0_rec_bb2, L0_rec_Wt0, L0_rec_bt0, L0_rec_Wt1, L0_rec_bt1, L0_rec_Wt2, L0_rec_bt2):
    import jax
    import jax.numpy as jnp

    def _L0_rec_ref(dense, sparse_idx, emb, Wb0, bb0, Wb1, bb1, Wb2, bb2, Wt0, bt0, Wt1, bt1, Wt2, bt2):
        import jax, jax.numpy as jnp
        import numpy as np
        NUM_TABLES = 26
        VOCAB = 12500
        M_SPA = 64
        N_DENSE = 13
        LN_BOT = [512, 256, 64]
        LN_TOP = [512, 256, 1]
        BATCH = 2048

        def _dense_params(key, dims):
            Ws, bs = ([], [])
            for i in range(len(dims) - 1):
                key, k = jax.random.split(key)
                fan_in = dims[i]
                Ws.append(jax.random.normal(k, (dims[i], dims[i + 1]), jnp.float32) / np.sqrt(fan_in))
                bs.append(jnp.zeros((dims[i + 1],), jnp.float32))
            return (Ws, bs)
        x = jax.nn.relu(dense @ Wb0 + bb0)
        x = jax.nn.relu(x @ Wb1 + bb1)
        d = jax.nn.relu(x @ Wb2 + bb2)
        sp = emb[jnp.arange(NUM_TABLES)[None, :], sparse_idx]
        T = jnp.concatenate([sp, d[:, None, :]], axis=1)
        Z = jnp.einsum('bnd,bmd->bnm', T, T)
        li, lj = np.tril_indices(NUM_TABLES + 1, -1)
        inter = Z[:, li, lj]
        h = jnp.concatenate([d, inter], axis=1)
        h = jax.nn.relu(h @ Wt0 + bt0)
        h = jax.nn.relu(h @ Wt1 + bt1)
        p = jax.nn.sigmoid(h @ Wt2 + bt2)
        return p.reshape(-1)
    y = _L0_rec_ref(r_dense, r_sparse_idx, L0_rec_emb, L0_rec_Wb0, L0_rec_bb0, L0_rec_Wb1, L0_rec_bb1, L0_rec_Wb2, L0_rec_bb2, L0_rec_Wt0, L0_rec_bt0, L0_rec_Wt1, L0_rec_bt1, L0_rec_Wt2, L0_rec_bt2)
    return y

_drawn_inputs = setup_inputs


def setup_inputs(seed=0):
    import zlib

    import numpy as np

    out = dict(_drawn_inputs(seed))
    spreads = {'L0_rec_bb0': (0.0, 0.8),
     'L0_rec_bb1': (0.0, 0.8),
     'L0_rec_bb2': (0.0, 0.8),
     'L0_rec_bt0': (0.0, 0.1),
     'L0_rec_bt1': (0.0, 0.1)}
    factors = {'r_dense': 3.041,
     'L0_rec_emb': 8.0,
     'L0_rec_Wb0': 2.805,
     'L0_rec_Wb1': 2.71,
     'L0_rec_Wt2': 3.243}
    for name, (base, spread) in spreads.items():
        noise = np.random.default_rng([zlib.crc32(name.encode()), seed]).standard_normal(out[name].shape)
        drawn = base * np.exp(spread * noise) if base else spread * noise
        out[name] = jnp.asarray(drawn.astype(out[name].dtype))
    for name, factor in factors.items():
        out[name] = (out[name] * factor).astype(out[name].dtype)
    return out
```

```python
from contextlib import ExitStack

import concourse.bass as bass
from concourse import mybir
import numpy as np

ALU = mybir.AluOpType
ACT = mybir.ActivationFunctionType
F32 = mybir.dt.float32
I32 = mybir.dt.int32

P = 128
BATCH = 2048
TABLES = 26
VOCAB = 12500
DIM = 64
DENSE = 13
B0, B1 = 512, 256
T0, T1 = 512, 256
TILES = BATCH // P
BODIES = TILES // 2

VECS = TABLES + 1
DSLOT = TABLES
HALF = TABLES // 2
SLOTS = 32
DELTAS = (VECS - 1) // 2
WRAP = VECS + DELTAS
KD = 4
KTILES = 4
KROWS = KD * VECS
BIAS_ROW = VECS
D_ROW = 64

RUNS = [(0, 4), (4, 4), (8, 4), (12, 1)]
GROUPS = P // 4
BATCHES = 4
GB = GROUPS // BATCHES
GCOLS = 4 * VECS


def slot_table(s):
    return 2 * s if s < HALF else 2 * (s - HALF) + 1 if s < TABLES else TABLES


def top_row_order():
    order = np.full((KTILES, P), -1, np.int64)
    for delta in range(1, DELTAS + 1):
        for i in range(VECS):
            a, b = slot_table(i), slot_table((i + delta) % VECS)
            hi, lo = max(a, b), min(a, b)
            order[(delta - 1) // KD, (delta - 1) % KD * VECS + i] = DIM + hi * (hi - 1) // 2 + lo
    order[KTILES - 1, BIAS_ROW] = -2
    order[KTILES - 1, D_ROW:D_ROW + DIM] = np.arange(DIM)
    return order


def build(nc, dense, idx, emb, wb0, bb0, wb1, bb1, wb2, bb2, wt0, wt1, bt1, wt2, bt2, out):
    emb_rows = emb.rearrange("t v d -> (t v) d")

    with ExitStack() as ctx:
        def sb(name, shape, dt=F32):
            return ctx.enter_context(nc.sbuf_tensor(name, shape, dt))

        def ps(name, shape):
            return ctx.enter_context(nc.psum_tensor(name, shape, F32))

        def sem(name):
            return ctx.enter_context(nc.semaphore(name))

        wb0_sb = sb("wb0_sb", [DENSE, B0])
        wb1_sb = sb("wb1_sb", [P, B0 // P, B1])
        wb2_sb = sb("wb2_sb", [P, B1 // P, DIM])
        wt0_sb = sb("wt0_sb", [P, KTILES, T0])
        wt1_sb = sb("wt1_sb", [P, T0 // P, T1])
        bb0_sb = sb("bb0_sb", [P, B0 // P])
        bb1_sb = sb("bb1_sb", [P, B1 // P])
        bb2_sb = sb("bb2_sb", [DIM, 1])
        bt1_sb = sb("bt1_sb", [1, T1])
        wt2_sb = sb("wt2_sb", [P, T1])
        bt2_sb = sb("bt2_sb", [P, 1])
        ident = sb("ident", [P, P])
        ones = sb("ones", [P, P])
        idx_raw = sb("idx_raw", [P, TILES * TABLES], I32)
        idx_neg = sb("idx_neg", [P, TILES * TABLES], I32)
        idx_base = sb("idx_base", [P, TILES * TABLES], I32)
        idx_row = sb("idx_row", [P, (TILES + 2) * TABLES], I32)
        idx_tile = [sb(f"idx_tile{q}", [P, TABLES], I32) for q in range(2)]
        x_sb = sb("x_sb", [P, TILES * DENSE])
        x_t = sb("x_t", [DENSE, TILES * P])
        hb0 = sb("hb0", [P, B0 // P, 2 * P])
        hb1 = sb("hb1", [P, B1 // P, 2 * P])
        rows = [sb(f"rows{q}", [P, TABLES * DIM]) for q in range(2)]
        vecs_t = [sb(f"vecs_t{q}", [DIM, GROUPS, 4, SLOTS]) for q in range(2)]
        gram_c = sb("gram_c", [P, VECS, GROUPS])
        gram_s = sb("gram_s", [P, WRAP * SLOTS])
        feat = sb("feat", [P, DELTAS * VECS])
        feat_t = [sb(f"feat_t{q}", [P, KTILES, P]) for q in range(2)]
        ht0 = sb("ht0", [P, T0])
        ht0_t = sb("ht0_t", [P, T0 // P, P])
        ht1 = sb("ht1", [P, T1])
        logits = sb("logits", [P, TILES])
        probs = sb("probs", [P, TILES])

        ps_gram = [ps(f"ps_gram{b}", [P, 2, 512]) for b in range(2)]
        ps_turn = [ps(f"ps_turn{b}", [P, 4, P]) for b in range(2)]
        ps_t0 = ps("ps_t0", [P, T0])
        ps_t1 = ps("ps_t1", [P, 512])

        idx_loaded = sem("idx_loaded")
        x_loaded = sem("x_loaded")
        bottom_loaded = sem("bottom_loaded")
        top_loaded = sem("top_loaded")
        base_ready = sem("base_ready")
        filled = sem("filled")
        ident_ready = sem("ident_ready")
        pads_ready = sem("pads_ready")
        idx_step = sem("idx_step")
        idx_staged = [sem(f"idx_staged{q}") for q in range(2)]
        rows_landed = [[sem(f"rows_landed{q}_{r}") for r in range(len(RUNS))] for q in range(2)]
        gathers_begun = sem("gathers_begun")
        rows_turned = sem("rows_turned")
        x_turned = sem("x_turned")
        x_act = sem("x_act")
        x_dve = sem("x_dve")
        b0_summed = sem("b0_summed")
        b0_act = sem("b0_act")
        b0_dve = sem("b0_dve")
        b1_summed = sem("b1_summed")
        b1_act = sem("b1_act")
        b1_dve = sem("b1_dve")
        b2_summed = sem("b2_summed")
        d_ready = sem("d_ready")
        vecs_act = sem("vecs_act")
        vecs_dve = sem("vecs_dve")
        gram_summed = sem("gram_summed")
        gram_act = sem("gram_act")
        gram_dve = sem("gram_dve")
        gram_s_ready = sem("gram_s_ready")
        feat_packed = sem("feat_packed")
        feat_turned = sem("feat_turned")
        feat_act = sem("feat_act")
        feat_dve = sem("feat_dve")
        t0_summed = sem("t0_summed")
        t0_act = sem("t0_act")
        t0_turned = sem("t0_turned")
        t0_dve = sem("t0_dve")
        t1_summed = sem("t1_summed")
        logit_ready = sem("logit_ready")
        probs_ready = sem("probs_ready")
        out_stored = sem("out_stored")

        block = ctx.enter_context(nc.Block())

        @block.sync
        def _(sp):
            sp.dma_start(idx_raw[:, :], idx.rearrange("(p n) t -> p (n t)", p=P)).then_inc(idx_loaded, 16)
            sp.dma_start(wb0_sb[:, :], wb0).then_inc(bottom_loaded, 16)
            sp.dma_start(wb1_sb[:, :, :], wb1.rearrange("(k p) n -> p k n", p=P)).then_inc(bottom_loaded, 16)
            sp.dma_start(wb2_sb[:, :, :], wb2.rearrange("(k p) n -> p k n", p=P)).then_inc(bottom_loaded, 16)
            sp.dma_start(wt0_sb[:, :, :], wt0.rearrange("k p n -> p k n")).then_inc(top_loaded, 16)
            sp.dma_start(wt1_sb[:, :, :], wt1.rearrange("(k p) n -> p k n", p=P)).then_inc(top_loaded, 16)
            sp.wait_ge(probs_ready, 1)
            sp.dma_start(out.rearrange("(p n) -> p n", p=P), probs[:, :]).then_inc(out_stored, 16)
            sp.wait_ge(out_stored, 16)

        @block.gpsimd
        def _(pool):
            nc.gpsimd.iota(idx_base[:, :], [[0, TILES], [VOCAB, TABLES]], base=0,
                           channel_multiplier=0).then_inc(base_ready, 1)
            pool.wait_ge(filled, 1)
            nc.gpsimd.affine_select(out=ident[:, :], in_=ones[:, :], pattern=[[-1, P]], compare_op=ALU.is_equal,
                                    fill=0.0, base=0, channel_multiplier=1).then_inc(ident_ready, 1)
            pool.sem_inc(rows_turned, 2 * len(RUNS))
            with pool.Fori(0, BODIES) as i:
                for q in range(2):
                    pool.wait_ge(idx_staged[q], i + 1)
                    pool.wait_ge(rows_turned, (i * 2 + (q + 1)) * len(RUNS))
                    pool.sem_inc(gathers_begun, 1)
                    for r, (first, pairs) in enumerate(RUNS):
                        for t in range(2 * first, 2 * (first + pairs)):
                            nc.gpsimd.indirect_dma_start(
                                rows[q][:, t * DIM:(t + 1) * DIM], None, emb_rows,
                                bass.IndirectOffsetOnAxis(idx_tile[q][:, t:t + 1], 0),
                            ).then_inc(rows_landed[q][r], 16)

        @block.tensor
        def _(pe):
            pe.wait_ge(ident_ready, 1)
            pe.wait_ge(x_loaded, 16)
            for n in range(TILES):
                turned = nc.tensor.transpose(
                    ps_gram[n // 8][0:DENSE, n % 8 // 4, n % 4 * P:(n % 4 + 1) * P],
                    x_sb[:, n * DENSE:(n + 1) * DENSE], ident[:, :])
                if n % 8 == 7:
                    turned.then_inc(x_turned, 1)
            pe.wait_ge(bottom_loaded, 16 * 6)
            pe.wait_ge(top_loaded, 16 * 5)
            pe.wait_ge(x_act, 1)
            pe.wait_ge(x_dve, 1)
            pe.wait_ge(pads_ready, 4)

            with pe.Fori(0, BODIES) as i:
                for m in range(B0 // P):
                    summed = nc.tensor.matmul(ps_gram[0][:, m // 2, m % 2 * 2 * P:(m % 2 + 1) * 2 * P],
                                              wb0_sb[:, m * P:(m + 1) * P], x_t[:, bass.ds(i * (2 * P), 2 * P)],
                                              start=True, stop=True)
                    if m % 2:
                        summed.then_inc(b0_summed, 1)
                pe.wait_ge(b0_act, i * 2 + 2)
                pe.wait_ge(b0_dve, i * 2 + 2)
                for m in range(B1 // P):
                    for k in range(B0 // P):
                        summed = nc.tensor.matmul(ps_gram[1][:, m, 0:2 * P],
                                                  wb1_sb[:, k, m * P:(m + 1) * P], hb0[:, k, :],
                                                  start=(k == 0), stop=(k == B0 // P - 1))
                    summed.then_inc(b1_summed, 1)
                pe.wait_ge(b1_act, i + 1)
                pe.wait_ge(b1_dve, i + 1)
                for k in range(B1 // P):
                    summed = nc.tensor.matmul(ps_gram[0][0:DIM, 0, 0:2 * P], wb2_sb[:, k, :], hb1[:, k, :],
                                              start=(k == 0), stop=(k == B1 // P - 1))
                summed.then_inc(b2_summed, 1)

                for q in range(2):
                    for r, (first, pairs) in enumerate(RUNS):
                        pe.wait_ge(rows_landed[q][r], (i + 1) * (32 * pairs))
                        if r >= 2:
                            pe.wait_ge(vecs_act, i * 8 + 4 * q + r - 1)
                            pe.wait_ge(vecs_dve, i * 8 + 4 * q + r - 1)
                        for j in range(pairs):
                            c = (first + j) * 2 * DIM
                            turned = nc.tensor.transpose(ps_turn[r % 2][:, j, :], rows[q][:, c:c + 2 * DIM],
                                                         ident[:, :])
                        turned.then_inc(rows_turned, 1)
                    pe.wait_ge(vecs_act, i * 8 + 4 * q + 4)
                    pe.wait_ge(vecs_dve, i * 8 + 4 * q + 4)
                    if q == 0:
                        pe.wait_ge(d_ready, i + 1)
                    for b in range(BATCHES):
                        if b >= 2:
                            pe.wait_ge(gram_act, i * 8 + 4 * q + b - 1)
                            pe.wait_ge(gram_dve, i * 8 + 4 * q + b - 1)
                        for g in range(GB):
                            v = vecs_t[q][:, b * GB + g]
                            c = g % 4 * GCOLS
                            summed = nc.tensor.matmul(
                                ps_gram[b % 2][:, g // 4, c:c + GCOLS].rearrange("p (s v) -> p s v", s=4),
                                v, v[:, :, 0:VECS], start=True, stop=True)
                        summed.then_inc(gram_summed, 1)
                    pe.wait_ge(feat_packed, i * 2 + q + 1)
                    for k in range(KTILES):
                        nd = min(KD, DELTAS - k * KD)
                        turned = nc.tensor.transpose(ps_turn[k // 3][0:nd * VECS, k % 3, :],
                                                     feat[:, k * KROWS:k * KROWS + nd * VECS], ident[:, :])
                    turned.then_inc(feat_turned, 1)
                    pe.wait_ge(feat_act, i * 2 + q + 1)
                    pe.wait_ge(feat_dve, i * 2 + q + 1)
                    for k in range(KTILES):
                        rows_k = KROWS if k < KTILES - 1 else P
                        summed = nc.tensor.matmul(ps_t0[:, :], feat_t[q][0:rows_k, k, :], wt0_sb[0:rows_k, k, :],
                                                  start=(k == 0), stop=(k == KTILES - 1))
                    summed.then_inc(t0_summed, 1)
                    pe.wait_ge(t0_act, i * 2 + q + 1)
                    for k in range(T0 // P):
                        turned = nc.tensor.transpose(ps_turn[1][:, k, :], ht0[:, k * P:(k + 1) * P], ident[:, :])
                    turned.then_inc(t0_turned, 1)
                    nc.tensor.matmul(ps_t1[:, 0:T1], ones[0:1, :], bt1_sb[:, :], start=True, stop=False)
                    pe.wait_ge(t0_dve, i * 2 + q + 1)
                    for k in range(T0 // P):
                        summed = nc.tensor.matmul(ps_t1[:, 0:T1], ht0_t[:, k, :], wt1_sb[:, k, :],
                                                  start=False, stop=(k == T0 // P - 1))
                    summed.then_inc(t1_summed, 1)

        @block.scalar
        def _(act):
            act.dma_start(x_sb[:, :], dense.rearrange("(p n) f -> p (n f)", p=P)).then_inc(x_loaded, 16)
            act.dma_start(bb0_sb[:, :], bb0).then_inc(bottom_loaded, 16)
            act.dma_start(bb1_sb[:, :], bb1).then_inc(bottom_loaded, 16)
            act.dma_start(bb2_sb[:, :], bb2).then_inc(bottom_loaded, 16)
            act.dma_start(bt1_sb[:, :], bt1).then_inc(top_loaded, 16)
            act.dma_start(wt2_sb[:, :], wt2.partition_broadcast(P)).then_inc(top_loaded, 16)
            act.dma_start(bt2_sb[:, :], bt2.partition_broadcast(P)).then_inc(top_loaded, 16)
            act.wait_ge(x_turned, 1)
            nc.scalar.activation(x_t[:, 0:8 * P], ps_gram[0][0:DENSE, :, :].rearrange("p a c -> p (a c)"),
                                 ACT.Copy).then_inc(x_act, 1)
            act.wait_ge(bottom_loaded, 16 * 6)
            act.wait_ge(top_loaded, 16 * 5)
            act.wait_ge(pads_ready, 4)

            with act.Fori(0, BODIES) as i:
                act.wait_ge(b0_summed, i * 2 + 1)
                for m in range(2):
                    nc.scalar.activation(hb0[:, m, :], ps_gram[0][:, 0, m * 2 * P:(m + 1) * 2 * P], ACT.Relu,
                                         bias=bb0_sb[:, m:m + 1]).then_inc(b0_act, 1)
                act.wait_ge(b1_summed, i * 2 + 1)
                nc.scalar.activation(hb1[:, 0, :], ps_gram[1][:, 0, 0:2 * P], ACT.Relu,
                                     bias=bb1_sb[:, 0:1]).then_inc(b1_act, 1)
                act.wait_ge(b2_summed, i + 1)
                for q in range(2):
                    d_sum = ps_gram[0][0:DIM, 0, q * P:(q + 1) * P]
                    nc.scalar.activation(vecs_t[q][:, :, :, DSLOT].rearrange("d g s -> d s g"),
                                         d_sum.rearrange("d (s g) -> d s g", s=4), ACT.Relu, bias=bb2_sb[:, 0:1])
                    last = nc.scalar.activation(feat_t[q][D_ROW:D_ROW + DIM, KTILES - 1, :], d_sum, ACT.Relu,
                                                bias=bb2_sb[:, 0:1])
                last.then_inc(d_ready, 1)

                for q in range(2):
                    for r, (first, pairs) in enumerate(RUNS):
                        act.wait_ge(rows_turned, i * 8 + 4 * q + r + 1 + 2 * len(RUNS))
                        for s in range(4):
                            moved = nc.scalar.activation(
                                vecs_t[q][:, :, s, first:first + pairs],
                                ps_turn[r % 2][0:DIM, 0:pairs, 32 * s:32 * s + 32].rearrange("d t g -> d g t"),
                                ACT.Copy)
                        moved.then_inc(vecs_act, 1)
                    for b in range(BATCHES):
                        act.wait_ge(gram_summed, i * 8 + 4 * q + b + 1)
                        for s in range(2):
                            moved = nc.scalar.activation(
                                gram_c[32 * s:32 * s + 32, :, b * GB:(b + 1) * GB]
                                .rearrange("p v (a g) -> p a g v", a=2),
                                ps_gram[b % 2][32 * s:32 * s + 32, :, 0:4 * GCOLS]
                                .rearrange("p a (g c) -> p a g c", g=4)[:, :, :, s * VECS:(s + 1) * VECS],
                                ACT.Copy)
                        moved.then_inc(gram_act, 1)
                    act.wait_ge(gram_s_ready, i * 4 + 2 * q + 2)
                    nc.scalar.activation(feat[:, :].rearrange("p (e i) -> p e i", e=DELTAS),
                                         bass.AP(gram_s, SLOTS, [[WRAP * SLOTS, P], [SLOTS, DELTAS], [SLOTS + 1, VECS]]),
                                         ACT.Copy).then_inc(feat_packed, 1)
                    act.wait_ge(feat_turned, i * 2 + q + 1)
                    nc.scalar.activation(feat_t[q][0:KROWS, 0:KTILES - 1, :], ps_turn[0][0:KROWS, 0:KTILES - 1, :],
                                         ACT.Copy).then_inc(feat_act, 1)
                    act.wait_ge(t0_summed, i * 2 + q + 1)
                    nc.scalar.activation(ht0[:, :], ps_t0[:, :], ACT.Relu).then_inc(t0_act, 1)
            act.wait_ge(logit_ready, TILES)
            nc.scalar.activation(probs[:, :], logits[:, :], ACT.Sigmoid, bias=bt2_sb[:, 0:1]).then_inc(probs_ready, 1)

        @block.vector
        def _(dve):
            nc.vector.memset(ones[:, :], 1.0).then_inc(filled, 1)
            dve.wait_ge(idx_loaded, 16)
            nc.vector.tensor_scalar(idx_neg[:, :], idx_raw[:, :], 0, VOCAB, ALU.is_lt, ALU.mult).then_inc(idx_step, 1)
            dve.wait_ge(idx_step, 1)
            nc.vector.tensor_tensor(idx_raw[:, :], idx_raw[:, :], idx_neg[:, :], ALU.add).then_inc(idx_step, 1)
            dve.wait_ge(idx_step, 2)
            nc.vector.tensor_scalar(idx_raw[:, :], idx_raw[:, :], 0, VOCAB - 1, ALU.max, ALU.min).then_inc(idx_step, 1)
            dve.wait_ge(idx_step, 3)
            dve.wait_ge(base_ready, 1)
            nc.vector.tensor_tensor(idx_row[:, 0:TILES * TABLES], idx_raw[:, :], idx_base[:, :],
                                    ALU.add).then_inc(idx_step, 1)
            nc.vector.memset(idx_row[:, TILES * TABLES:(TILES + 2) * TABLES], 0).then_inc(idx_step, 1)
            dve.wait_ge(idx_step, 5)
            for q in range(2):
                nc.vector.tensor_copy(idx_tile[q][:, :], idx_row[:, q * TABLES:(q + 1) * TABLES])\
                    .then_inc(idx_staged[q], 1)
            for q in range(2):
                nc.vector.memset(vecs_t[q][:, :, :, VECS:SLOTS], 0.0).then_inc(pads_ready, 1)
                nc.vector.memset(feat_t[q][:, KTILES - 1, :], 1.0).then_inc(pads_ready, 1)
            dve.wait_ge(x_turned, 2)
            nc.vector.tensor_copy(x_t[:, 8 * P:16 * P], ps_gram[1][0:DENSE, :, :].rearrange("p a c -> p (a c)"))\
                .then_inc(x_dve, 1)

            dve.wait_ge(bottom_loaded, 16 * 6)
            dve.wait_ge(top_loaded, 16 * 5)
            with dve.Fori(0, BODIES) as i:
                dve.wait_ge(b0_summed, i * 2 + 2)
                for m in range(2, 4):
                    nc.vector.tensor_scalar(hb0[:, m, :], ps_gram[0][:, 1, (m - 2) * 2 * P:(m - 1) * 2 * P],
                                            bb0_sb[:, m:m + 1], 0.0, ALU.add, ALU.max).then_inc(b0_dve, 1)
                dve.wait_ge(b1_summed, i * 2 + 2)
                nc.vector.tensor_scalar(hb1[:, 1, :], ps_gram[1][:, 1, 0:2 * P], bb1_sb[:, 1:2], 0.0,
                                        ALU.add, ALU.max).then_inc(b1_dve, 1)

                for q in range(2):
                    for r, (first, pairs) in enumerate(RUNS):
                        dve.wait_ge(rows_turned, i * 8 + 4 * q + r + 1 + 2 * len(RUNS))
                        for s in range(4):
                            moved = nc.vector.tensor_copy(
                                vecs_t[q][:, :, s, HALF + first:HALF + first + pairs],
                                ps_turn[r % 2][DIM:P, 0:pairs, 32 * s:32 * s + 32].rearrange("d t g -> d g t"))
                        moved.then_inc(vecs_dve, 1)
                    for r, (first, pairs) in enumerate(RUNS):
                        dve.wait_ge(rows_landed[q][r], (i + 1) * (32 * pairs))
                    nc.vector.tensor_copy(idx_tile[q][:, :], idx_row[:, bass.ds(i * (2 * TABLES) + (q + 2) * TABLES, TABLES)])\
                        .then_inc(idx_staged[q], 1)
                    for b in range(BATCHES):
                        dve.wait_ge(gram_summed, i * 8 + 4 * q + b + 1)
                        for s in range(2, 4):
                            moved = nc.vector.tensor_copy(
                                gram_c[32 * s:32 * s + 32, :, b * GB:(b + 1) * GB]
                                .rearrange("p v (a g) -> p a g v", a=2),
                                ps_gram[b % 2][32 * s:32 * s + 32, :, 0:4 * GCOLS]
                                .rearrange("p a (g c) -> p a g c", g=4)[:, :, :, s * VECS:(s + 1) * VECS])
                        moved.then_inc(gram_dve, 1)
                    dve.wait_ge(gram_act, i * 8 + 4 * q + 4)
                    dve.wait_ge(gram_dve, i * 8 + 4 * q + 4)
                    nc.vector.transpose(gram_s[:, 0:VECS * SLOTS], gram_c[:, :, :].rearrange("p v g -> p (v g)"))\
                        .then_inc(gram_s_ready, 1)
                    nc.vector.transpose(gram_s[:, VECS * SLOTS:WRAP * SLOTS],
                                        gram_c[:, 0:DELTAS, :].rearrange("p v g -> p (v g)"))\
                        .then_inc(gram_s_ready, 1)
                    dve.wait_ge(feat_turned, i * 2 + q + 1)
                    nc.vector.tensor_copy(feat_t[q][0:VECS, KTILES - 1, :], ps_turn[1][0:VECS, 0, :])\
                        .then_inc(feat_dve, 1)
                    dve.wait_ge(t0_turned, i * 2 + q + 1)
                    nc.vector.tensor_copy(ht0_t[:, :, :], ps_turn[1][:, :, :]).then_inc(t0_dve, 1)
                    dve.wait_ge(t1_summed, i * 2 + q + 1)
                    nc.vector.scalar_tensor_tensor(out=ht1[:, :], in0=ps_t1[:, 0:T1], scalar=0.0, in1=wt2_sb[:, :],
                                                   op0=ALU.max, op1=ALU.mult,
                                                   accum_out=logits[:, bass.ds(i * 2 + q, 1)]).then_inc(logit_ready, 1)


def kernel(**inputs):
    import concourse.bacc as bacc
    from concourse.bass_utils import run_bass_kernel_spmd as run

    def get(name):
        return np.ascontiguousarray(inputs[name])

    order = top_row_order()
    wt0_rows = np.concatenate([get("L0_rec_Wt0"), get("L0_rec_bt0").reshape(1, T0),
                               np.zeros((1, T0), np.float32)])
    arrays = {
        "dense": get("r_dense"),
        "idx": get("r_sparse_idx"),
        "emb": get("L0_rec_emb"),
        "wb0": get("L0_rec_Wb0"),
        "bb0": np.ascontiguousarray(get("L0_rec_bb0").reshape(B0 // P, P).T),
        "wb1": get("L0_rec_Wb1"),
        "bb1": np.ascontiguousarray(get("L0_rec_bb1").reshape(B1 // P, P).T),
        "wb2": get("L0_rec_Wb2"),
        "bb2": get("L0_rec_bb2").reshape(DIM, 1),
        "wt0": wt0_rows[np.where(order == -1, wt0_rows.shape[0] - 1, np.where(order == -2, wt0_rows.shape[0] - 2, order))],
        "wt1": get("L0_rec_Wt1"),
        "bt1": get("L0_rec_bt1").reshape(1, T1),
        "wt2": get("L0_rec_Wt2").reshape(T1),
        "bt2": get("L0_rec_bt2").reshape(1),
    }
    nc = bacc.Bacc("TRN2", target_bir_lowering=False, num_devices=1)
    args = [nc.dram_tensor("in_" + name, a.shape, mybir.dt.from_np(a.dtype), kind="ExternalInput").ap()
            for name, a in arrays.items()]
    out = nc.dram_tensor("out_0", (BATCH,), F32, kind="ExternalOutput").ap()
    build(nc, *args, out)
    result = run(nc, [{"in_" + name: a for name, a in arrays.items()}], core_ids=[0])
    return result.results[0]["out_0"]
```

```python
from contextlib import ExitStack

import concourse.bass as bass
from concourse import mybir
import numpy as np

ALU = mybir.AluOpType
ACT = mybir.ActivationFunctionType
F32 = mybir.dt.float32
I32 = mybir.dt.int32

P = 128
BATCH = 2048
TABLES = 26
VOCAB = 12500
DIM = 64
DENSE = 13
B0, B1 = 512, 256
T0, T1 = 512, 256
STEP = 2 * P
STEPS = BATCH // STEP

VECS = TABLES + 1
DSLOT = TABLES
SLOTS = 32
DELTAS = (VECS - 1) // 2
WRAP = VECS + DELTAS
KD = 4
KTILES = 4
KROWS = KD * VECS
BIAS_ROW = VECS
D_ROW = 64

RUNS = [(t, min(4, TABLES - t)) for t in range(0, TABLES, 4)]
NR = len(RUNS)
ACT_RUNS = (NR + 1) // 2
DVE_RUNS = NR // 2
HEAD = 4
HEAD_COLS = 2 * RUNS[HEAD][0]
STEP_COLS = 2 * TABLES

GROUPS = P // 2
BATCHES = 8
UB = BATCHES // 2
GB = GROUPS // BATCHES
GCOLS = 2 * VECS


def top_row_order():
    order = np.full((KTILES, P), -1, np.int64)
    for delta in range(1, DELTAS + 1):
        for i in range(VECS):
            j = (i + delta) % VECS
            hi, lo = max(i, j), min(i, j)
            order[(delta - 1) // KD, (delta - 1) % KD * VECS + i] = DIM + hi * (hi - 1) // 2 + lo
    order[KTILES - 1, BIAS_ROW] = -2
    order[KTILES - 1, D_ROW:D_ROW + DIM] = np.arange(DIM)
    return order


def build(nc, x, idx, emb, wb0, bb0, wb1, bb1, wb2, bb2, wt0, wt1, bt1, wt2, bt2, out):
    emb_rows = emb.rearrange("t v d -> (t v) d")

    with ExitStack() as ctx:
        def sb(name, shape, dt=F32):
            return ctx.enter_context(nc.sbuf_tensor(name, shape, dt))

        def ps(name, shape):
            return ctx.enter_context(nc.psum_tensor(name, shape, F32))

        def sem(name):
            return ctx.enter_context(nc.semaphore(name))

        wb0_sb = sb("wb0_sb", [DENSE, B0])
        wb1_sb = sb("wb1_sb", [P, B0 // P, B1])
        wb2_sb = sb("wb2_sb", [P, B1 // P, DIM])
        wt0_sb = sb("wt0_sb", [P, KTILES, T0])
        wt1_sb = sb("wt1_sb", [P, T0 // P, T1])
        bb0_sb = sb("bb0_sb", [P, B0 // P])
        bb1_sb = sb("bb1_sb", [P, B1 // P])
        bb2_sb = sb("bb2_sb", [DIM, 1])
        bt1_sb = sb("bt1_sb", [P, T1])
        wt2_sb = sb("wt2_sb", [P, T1])
        bt2_sb = sb("bt2_sb", [P, 1])
        ident = sb("ident", [P, P])
        ones = sb("ones", [P, P])
        idx_raw = sb("idx_raw", [P, STEPS * STEP_COLS], I32)
        idx_neg = sb("idx_neg", [P, STEPS * STEP_COLS], I32)
        idx_base = sb("idx_base", [P, STEPS * STEP_COLS], I32)
        idx_row = sb("idx_row", [P, STEPS * STEP_COLS], I32)
        idx_step = sb("idx_step", [P, STEP_COLS], I32)
        x_t = sb("x_t", [DENSE, BATCH])
        hb0 = sb("hb0", [P, B0 // P, STEP])
        hb1 = sb("hb1", [P, B1 // P, STEP])
        d_hold = sb("d_hold", [P, 2, P])
        rows = sb("rows", [P, TABLES, 2 * DIM])
        vecs_st = sb("vecs_st", [P, GROUPS, 2, 2, SLOTS])
        vecs_mv = sb("vecs_mv", [P, GROUPS, 2, VECS])
        gram_c = sb("gram_c", [P, 2, VECS, SLOTS])
        gram_s = [sb(f"gram_s{u}", [P, WRAP * SLOTS]) for u in range(2)]
        feat = sb("feat", [P, 2, DELTAS * VECS])
        feat_t = sb("feat_t", [P, 2, KTILES, P])
        ht0 = sb("ht0", [P, T0])
        ht0_t = sb("ht0_t", [P, T0 // P, P])
        ht1 = sb("ht1", [P, T1])
        ht1_w = sb("ht1_w", [P, T1])
        logits = sb("logits", [P, 2 * STEPS])
        probs = sb("probs", [P, 2 * STEPS])

        ps_turn = [ps(f"ps_turn{b}", [P, 4, P]) for b in range(2)]
        ps_gram = [ps(f"ps_gram{b}", [P, 512]) for b in range(2)]
        ps_feat = [ps(f"ps_feat{u}", [P, 4, P]) for u in range(2)]
        ps_t0 = ps("ps_t0", [P, T0])
        ps_t1 = ps("ps_t1", [P, 512])

        idx_loaded = sem("idx_loaded")
        bottom_loaded = sem("bottom_loaded")
        top_loaded = sem("top_loaded")
        base_ready = sem("base_ready")
        filled = sem("filled")
        ident_ready = sem("ident_ready")
        pads_ready = sem("pads_ready")
        idx_done = sem("idx_done")
        head_staged = sem("head_staged")
        rest_staged = sem("rest_staged")
        gathers_begun = sem("gathers_begun")
        rows_landed = [sem(f"rows_landed{r}") for r in range(NR)]
        rows_turned = sem("rows_turned")
        b0_summed = sem("b0_summed")
        b0_act = sem("b0_act")
        b0_dve = sem("b0_dve")
        b1_summed = sem("b1_summed")
        b1_act = sem("b1_act")
        b1_dve = sem("b1_dve")
        b2_summed = sem("b2_summed")
        d_ready = sem("d_ready")
        d_copied = sem("d_copied")
        vecs_act = sem("vecs_act")
        vecs_dve = sem("vecs_dve")
        gram_summed = sem("gram_summed")
        gram_act = sem("gram_act")
        gram_dve = sem("gram_dve")
        gram_turned = sem("gram_turned")
        feat_packed = sem("feat_packed")
        feat_turned = sem("feat_turned")
        feat_act = sem("feat_act")
        feat_dve = sem("feat_dve")
        t0_summed = sem("t0_summed")
        t0_act = sem("t0_act")
        t0_turned = sem("t0_turned")
        t0_dve = sem("t0_dve")
        t1_summed = sem("t1_summed")
        t1_biased = sem("t1_biased")
        logit_ready = sem("logit_ready")
        probs_ready = sem("probs_ready")
        out_stored = sem("out_stored")

        def turned_rows(r):
            first, n = RUNS[r]
            bank = ps_turn[r % 2]
            yield (vecs_mv[:, :, :, first:first + n].rearrange("p g s t -> p s g t"),
                   bank[:, 0:n, :].rearrange("p t (s g) -> p s g t", s=2))
            for h in range(2):
                part = slice(DIM * h, DIM * (h + 1))
                yield (vecs_st[part, :, :, h, first:first + n].rearrange("p g s t -> p s g t"),
                       bank[part, 0:n, :].rearrange("p t (s g) -> p s g t", s=2))

        def gram_blocks(b, s):
            u, c = b // UB, b % UB * GB
            part = slice(DIM * s, DIM * (s + 1))
            return (gram_c[part, u, :, c:c + GB].rearrange("p v g -> p g v"),
                    ps_gram[b % 2][part, 0:GB * GCOLS].rearrange("p (g c) -> p g c", g=GB)
                    [:, :, s * VECS:(s + 1) * VECS])

        block = ctx.enter_context(nc.Block())

        @block.sync
        def _(sp):
            sp.dma_start(idx_raw[:, :], idx).then_inc(idx_loaded, 16)
            sp.dma_start(wb0_sb[:, :], wb0).then_inc(bottom_loaded, 16)
            sp.dma_start(wb1_sb[:, :, :], wb1.rearrange("(k p) n -> p k n", p=P)).then_inc(bottom_loaded, 16)
            sp.dma_start(wb2_sb[:, :, :], wb2.rearrange("(k p) n -> p k n", p=P)).then_inc(bottom_loaded, 16)
            sp.dma_start(wt0_sb[:, :, :], wt0.rearrange("k p n -> p k n")).then_inc(top_loaded, 16)
            sp.dma_start(wt1_sb[:, :, :], wt1.rearrange("(k p) n -> p k n", p=P)).then_inc(top_loaded, 16)
            sp.wait_ge(probs_ready, 1)
            sp.dma_start(out.rearrange("(p n) -> p n", p=P), probs[:, :]).then_inc(out_stored, 16)
            sp.wait_ge(out_stored, 16)

        @block.gpsimd
        def _(pool):
            nc.gpsimd.iota(idx_base[:, :], [[0, STEPS], [VOCAB, TABLES], [0, 2]], base=0,
                           channel_multiplier=0).then_inc(base_ready, 1)
            pool.wait_ge(filled, 1)
            nc.gpsimd.affine_select(out=ident[:, :], in_=ones[:, :], pattern=[[-1, P]], compare_op=ALU.is_equal,
                                    fill=0.0, base=0, channel_multiplier=1).then_inc(ident_ready, 1)
            pool.sem_inc(rows_turned, NR)
            with pool.Fori(0, STEPS) as i:
                for staged, lo, hi in ((head_staged, 0, HEAD), (rest_staged, HEAD, NR)):
                    pool.wait_ge(staged, i + 1)
                    pool.wait_ge(rows_turned, i * NR + hi)
                    pool.sem_inc(gathers_begun, 1)
                    for r in range(lo, hi):
                        first, n = RUNS[r]
                        for t in range(first, first + n):
                            for h in range(2):
                                c = 2 * t + h
                                nc.gpsimd.indirect_dma_start(
                                    rows[:, t, h * DIM:(h + 1) * DIM], None, emb_rows,
                                    bass.IndirectOffsetOnAxis(idx_step[:, c:c + 1], 0),
                                ).then_inc(rows_landed[r], 16)

        @block.tensor
        def _(pe):
            def bottom_0(i):
                for m in range(B0 // P):
                    summed = nc.tensor.matmul(ps_gram[m // 2][:, m % 2 * STEP:(m % 2 + 1) * STEP],
                                              wb0_sb[:, m * P:(m + 1) * P], x_t[:, bass.ds(i * STEP, STEP)],
                                              start=True, stop=True)
                    if m % 2:
                        summed.then_inc(b0_summed, 1)

            def bottom_12(i):
                pe.wait_ge(b0_act, i + 1)
                pe.wait_ge(b0_dve, i + 1)
                for m in range(B1 // P):
                    for k in range(B0 // P):
                        summed = nc.tensor.matmul((ps_t0, ps_t1)[m][:, 0:STEP], wb1_sb[:, k, m * P:(m + 1) * P],
                                                  hb0[:, k, :], start=(k == 0), stop=(k == B0 // P - 1))
                    summed.then_inc(b1_summed, 1)
                pe.wait_ge(b1_act, i + 1)
                pe.wait_ge(b1_dve, i + 1)
                for k in range(B1 // P):
                    summed = nc.tensor.matmul(ps_gram[0][0:DIM, 0:STEP], wb2_sb[:, k, :], hb1[:, k, :],
                                              start=(k == 0), stop=(k == B1 // P - 1))
                summed.then_inc(b2_summed, 1)

            def turn(i, r):
                first, n = RUNS[r]
                pe.wait_ge(rows_landed[r], (i + 1) * (32 * n))
                if r >= 2 and r % 2 == 0:
                    pe.wait_ge(vecs_act, i * ACT_RUNS + r // 2)
                if r >= 2 and r % 2 == 1:
                    pe.wait_ge(vecs_dve, i * DVE_RUNS + r // 2)
                for j in range(n):
                    turned = nc.tensor.transpose(ps_turn[r % 2][:, j, :], rows[:, first + j, :], ident[:, :])
                turned.then_inc(rows_turned, 1)

            def gram(i):
                pe.wait_ge(vecs_act, (i + 1) * ACT_RUNS)
                pe.wait_ge(vecs_dve, (i + 1) * DVE_RUNS)
                pe.wait_ge(d_ready, i + 1)
                for b in range(BATCHES):
                    if b >= 2:
                        pe.wait_ge(gram_act, i * BATCHES + b - 1)
                        pe.wait_ge(gram_dve, i * BATCHES + b - 1)
                    for g in range(GB):
                        summed = nc.tensor.matmul(
                            ps_gram[b % 2][:, g * GCOLS:(g + 1) * GCOLS],
                            vecs_st[:, b * GB + g].rearrange("p s h t -> p (s h t)"),
                            vecs_mv[:, b * GB + g].rearrange("p s t -> p (s t)"), start=True, stop=True)
                    summed.then_inc(gram_summed, 1)

            def turn_feat(i, u):
                pe.wait_ge(feat_packed, i * 2 + u + 1)
                for k in range(KTILES):
                    nd = min(KD, DELTAS - k * KD)
                    turned = nc.tensor.transpose(ps_feat[u][0:nd * VECS, k, :],
                                                 feat[:, u, k * KROWS:k * KROWS + nd * VECS], ident[:, :])
                turned.then_inc(feat_turned, 1)

            def top_0(i, u):
                if u == 0:
                    pe.wait_ge(feat_act, i + 1)
                    pe.wait_ge(d_copied, i + 1)
                else:
                    pe.wait_ge(feat_dve, i + 1)
                for k in range(KTILES):
                    rows_k = KROWS if k < KTILES - 1 else P
                    summed = nc.tensor.matmul(ps_t0[:, :], feat_t[0:rows_k, u, k, :], wt0_sb[0:rows_k, k, :],
                                              start=(k == 0), stop=(k == KTILES - 1))
                summed.then_inc(t0_summed, 1)

            def turn_top(i, u):
                pe.wait_ge(t0_act, i * 2 + u + 1)
                for k in range(T0 // P):
                    turned = nc.tensor.transpose(ps_feat[u][:, k, :], ht0[:, k * P:(k + 1) * P], ident[:, :])
                turned.then_inc(t0_turned, 1)

            def top_1(i, u):
                pe.wait_ge(t0_dve, i * 2 + u + 1)
                if u == 1:
                    pe.wait_ge(logit_ready, i * 2 + 1)
                for k in range(T0 // P):
                    summed = nc.tensor.matmul(ps_t1[:, 0:T1], ht0_t[:, k, :], wt1_sb[:, k, :],
                                              start=(k == 0), stop=(k == T0 // P - 1))
                summed.then_inc(t1_summed, 1)

            def step(i, top, bottom):
                turn(i, 0)
                if top:
                    top_0(i - 1, 0)
                turn(i, 1)
                if top:
                    turn_top(i - 1, 0)
                turn(i, 2)
                if top:
                    top_1(i - 1, 0)
                    top_0(i - 1, 1)
                turn(i, 3)
                if top:
                    turn_top(i - 1, 1)
                turn(i, 4)
                if top:
                    top_1(i - 1, 1)
                turn(i, 5)
                turn(i, 6)
                gram(i)
                turn_feat(i, 0)
                if bottom:
                    pe.wait_ge(gram_act, (i + 1) * BATCHES)
                    pe.wait_ge(gram_dve, (i + 1) * BATCHES)
                    bottom_0(i + 1)
                    turn_feat(i, 1)
                    bottom_12(i + 1)
                else:
                    top_0(i, 0)
                    turn_feat(i, 1)
                    turn_top(i, 0)
                    top_0(i, 1)
                    top_1(i, 0)
                    turn_top(i, 1)
                    top_1(i, 1)

            pe.wait_ge(bottom_loaded, 16 * 7)
            bottom_0(0)
            bottom_12(0)
            pe.wait_ge(ident_ready, 1)
            step(0, top=False, bottom=True)
            pe.wait_ge(top_loaded, 16 * 5)
            with pe.Fori(1, STEPS - 1) as i:
                step(i, top=True, bottom=True)
            step(STEPS - 1, top=True, bottom=False)

        @block.scalar
        def _(act):
            def bottom(i):
                act.wait_ge(b0_summed, i * 2 + 1)
                for m in range(2):
                    moved = nc.scalar.activation(hb0[:, m, :], ps_gram[0][:, m * STEP:(m + 1) * STEP], ACT.Relu,
                                                 bias=bb0_sb[:, m:m + 1])
                moved.then_inc(b0_act, 1)
                act.wait_ge(b1_summed, i * 2 + 1)
                nc.scalar.activation(hb1[:, 0, :], ps_t0[:, 0:STEP], ACT.Relu, bias=bb1_sb[:, 0:1]).then_inc(b1_act, 1)
                act.wait_ge(b2_summed, i + 1)
                for h in range(2):
                    d_sum = ps_gram[0][0:DIM, h * P:(h + 1) * P].rearrange("d (s g) -> d s g", s=2)
                    part = slice(DIM * h, DIM * (h + 1))
                    nc.scalar.activation(vecs_mv[part, :, :, DSLOT].rearrange("d g s -> d s g"), d_sum, ACT.Relu,
                                         bias=bb2_sb[:, 0:1])
                    nc.scalar.activation(vecs_st[part, :, :, h, DSLOT].rearrange("d g s -> d s g"), d_sum, ACT.Relu,
                                         bias=bb2_sb[:, 0:1])
                for u in range(2):
                    d_sum = ps_gram[0][0:DIM, 0:STEP].rearrange("d (h s u g) -> d u s h g", h=2, s=2, u=2)[:, u]
                    moved = nc.scalar.activation(d_hold[D_ROW:P, u, :].rearrange("d (s h g) -> d s h g", s=2, h=2),
                                                 d_sum, ACT.Relu, bias=bb2_sb[:, 0:1])
                moved.then_inc(d_ready, 1)

            def spread(i, r):
                act.wait_ge(rows_turned, i * NR + r + 1 + NR)
                for to, source in turned_rows(r):
                    moved = nc.scalar.activation(to, source, ACT.Copy)
                moved.then_inc(vecs_act, 1)

            def blocks(i, b):
                act.wait_ge(gram_summed, i * BATCHES + b + 1)
                nc.scalar.activation(*gram_blocks(b, 0), ACT.Copy).then_inc(gram_act, 1)

            def pack(i, u):
                act.wait_ge(gram_turned, i * 4 + 2 * u + 2)
                nc.scalar.activation(feat[:, u, :].rearrange("p (e i) -> p e i", e=DELTAS),
                                     bass.AP(gram_s[u], SLOTS, [[WRAP * SLOTS, P], [SLOTS, DELTAS], [SLOTS + 1, VECS]]),
                                     ACT.Copy).then_inc(feat_packed, 1)

            def relu_top(i, u):
                act.wait_ge(t0_summed, i * 2 + u + 1)
                nc.scalar.activation(ht0[:, :], ps_t0[:, :], ACT.Relu).then_inc(t0_act, 1)

            def step(i, top, do_bottom):
                spread(i, 0)
                if top:
                    relu_top(i - 1, 0)
                spread(i, 2)
                if top:
                    relu_top(i - 1, 1)
                spread(i, 4)
                spread(i, 6)
                act.wait_ge(d_ready, i + 1)
                nc.scalar.activation(feat_t[D_ROW:P, :, KTILES - 1, :], d_hold[D_ROW:P, :, :], ACT.Copy)\
                    .then_inc(d_copied, 1)
                for b in range(BATCHES - 1):
                    blocks(i, b)
                pack(i, 0)
                blocks(i, BATCHES - 1)
                act.wait_ge(feat_turned, i * 2 + 1)
                nc.scalar.activation(feat_t[0:VECS, 0, KTILES - 1, :], ps_feat[0][0:VECS, KTILES - 1, :], ACT.Copy)
                nc.scalar.activation(feat_t[0:KROWS, 0, 0:KTILES - 1, :], ps_feat[0][0:KROWS, 0:KTILES - 1, :],
                                     ACT.Copy).then_inc(feat_act, 1)
                pack(i, 1)
                if do_bottom:
                    bottom(i + 1)
                else:
                    relu_top(i, 0)
                    relu_top(i, 1)

            act.dma_start(x_t[:, :], x).then_inc(bottom_loaded, 16)
            act.dma_start(bb0_sb[:, :], bb0).then_inc(bottom_loaded, 16)
            act.dma_start(bb1_sb[:, :], bb1).then_inc(bottom_loaded, 16)
            act.dma_start(bb2_sb[:, :], bb2).then_inc(bottom_loaded, 16)
            act.dma_start(bt1_sb[:, :], bt1.partition_broadcast(P)).then_inc(top_loaded, 16)
            act.dma_start(wt2_sb[:, :], wt2.partition_broadcast(P)).then_inc(top_loaded, 16)
            act.dma_start(bt2_sb[:, :], bt2.partition_broadcast(P)).then_inc(top_loaded, 16)
            act.wait_ge(bottom_loaded, 16 * 7)
            act.wait_ge(pads_ready, 2)
            bottom(0)
            step(0, top=False, do_bottom=True)
            with act.Fori(1, STEPS - 1) as i:
                step(i, top=True, do_bottom=True)
            step(STEPS - 1, top=True, do_bottom=False)
            act.wait_ge(top_loaded, 16 * 5)
            act.wait_ge(logit_ready, 2 * STEPS)
            nc.scalar.activation(probs[:, :], logits[:, :], ACT.Sigmoid, bias=bt2_sb[:, 0:1]).then_inc(probs_ready, 1)

        @block.vector
        def _(dve):
            def stage(i, staged, lo, hi, runs):
                for r in runs:
                    dve.wait_ge(rows_landed[r], (i + 1) * (32 * RUNS[r][1]))
                nc.vector.tensor_copy(idx_step[:, lo:hi], idx_row[:, bass.ds(i * STEP_COLS + (STEP_COLS + lo), hi - lo)])\
                    .then_inc(staged, 1)

            def bottom(i):
                dve.wait_ge(b0_summed, i * 2 + 2)
                for m in range(2, 4):
                    moved = nc.vector.tensor_scalar(hb0[:, m, :], ps_gram[1][:, (m - 2) * STEP:(m - 1) * STEP],
                                                    bb0_sb[:, m:m + 1], 0.0, ALU.add, ALU.max)
                moved.then_inc(b0_dve, 1)
                dve.wait_ge(b1_summed, i * 2 + 2)
                nc.vector.tensor_scalar(hb1[:, 1, :], ps_t1[:, 0:STEP], bb1_sb[:, 1:2], 0.0,
                                        ALU.add, ALU.max).then_inc(b1_dve, 1)

            def spread(i, r):
                dve.wait_ge(rows_turned, i * NR + r + 1 + NR)
                for to, source in turned_rows(r):
                    moved = nc.vector.tensor_copy(to, source)
                moved.then_inc(vecs_dve, 1)

            def blocks(i, b):
                dve.wait_ge(gram_summed, i * BATCHES + b + 1)
                nc.vector.tensor_copy(*gram_blocks(b, 1)).then_inc(gram_dve, 1)

            def turn_gram(i, u, wrap):
                if not wrap:
                    dve.wait_ge(gram_act, i * BATCHES + UB * (u + 1))
                    dve.wait_ge(gram_dve, i * BATCHES + UB * (u + 1))
                    to, n = gram_s[u][:, 0:VECS * SLOTS], VECS
                else:
                    to, n = gram_s[u][:, VECS * SLOTS:WRAP * SLOTS], DELTAS
                nc.vector.transpose(to, gram_c[:, u, 0:n, :].rearrange("p v g -> p (v g)")).then_inc(gram_turned, 1)

            def move_top(i, u):
                dve.wait_ge(t0_turned, i * 2 + u + 1)
                nc.vector.tensor_copy(ht0_t[:, :, :], ps_feat[u][:, :, :]).then_inc(t0_dve, 1)

            def logit(i, u):
                dve.wait_ge(t1_summed, i * 2 + u + 1)
                nc.vector.tensor_tensor(ht1[:, :], ps_t1[:, 0:T1], bt1_sb[:, :], ALU.add).then_inc(t1_biased, 1)
                dve.wait_ge(t1_biased, i * 2 + u + 1)
                nc.vector.scalar_tensor_tensor(out=ht1_w[:, :], in0=ht1[:, :], scalar=0.0, in1=wt2_sb[:, :],
                                               op0=ALU.max, op1=ALU.mult,
                                               accum_out=logits[:, bass.ds(i * 2 + u, 1)]).then_inc(logit_ready, 1)

            def step(i, top, do_bottom):
                spread(i, 1)
                if top:
                    move_top(i - 1, 0)
                    logit(i - 1, 0)
                spread(i, 3)
                if do_bottom:
                    stage(i, head_staged, 0, HEAD_COLS, range(HEAD))
                if top:
                    move_top(i - 1, 1)
                    logit(i - 1, 1)
                spread(i, 5)
                for b in range(UB + 1):
                    blocks(i, b)
                turn_gram(i, 0, wrap=False)
                blocks(i, UB + 1)
                turn_gram(i, 0, wrap=True)
                if do_bottom:
                    stage(i, rest_staged, HEAD_COLS, STEP_COLS, range(HEAD, NR))
                for b in range(UB + 2, BATCHES):
                    blocks(i, b)
                turn_gram(i, 1, wrap=False)
                turn_gram(i, 1, wrap=True)
                if do_bottom:
                    dve.wait_ge(b0_summed, (i + 1) * 2 + 2)
                    for m in range(2, 4):
                        moved = nc.vector.tensor_scalar(hb0[:, m, :], ps_gram[1][:, (m - 2) * STEP:(m - 1) * STEP],
                                                        bb0_sb[:, m:m + 1], 0.0, ALU.add, ALU.max)
                    moved.then_inc(b0_dve, 1)
                dve.wait_ge(feat_turned, i * 2 + 2)
                nc.vector.tensor_copy(feat_t[0:VECS, 1, KTILES - 1, :], ps_feat[1][0:VECS, KTILES - 1, :])
                nc.vector.tensor_copy(feat_t[0:KROWS, 1, 0:KTILES - 1, :], ps_feat[1][0:KROWS, 0:KTILES - 1, :])\
                    .then_inc(feat_dve, 1)
                if do_bottom:
                    dve.wait_ge(b1_summed, (i + 1) * 2 + 2)
                    nc.vector.tensor_scalar(hb1[:, 1, :], ps_t1[:, 0:STEP], bb1_sb[:, 1:2], 0.0,
                                            ALU.add, ALU.max).then_inc(b1_dve, 1)
                else:
                    move_top(i, 0)
                    logit(i, 0)
                    move_top(i, 1)
                    logit(i, 1)

            nc.vector.memset(ones[:, :], 1.0).then_inc(filled, 1)
            dve.wait_ge(idx_loaded, 16)
            nc.vector.tensor_scalar(idx_neg[:, :], idx_raw[:, :], 0, VOCAB, ALU.is_lt, ALU.mult).then_inc(idx_done, 1)
            dve.wait_ge(idx_done, 1)
            nc.vector.tensor_tensor(idx_raw[:, :], idx_raw[:, :], idx_neg[:, :], ALU.add).then_inc(idx_done, 1)
            dve.wait_ge(idx_done, 2)
            nc.vector.tensor_scalar(idx_raw[:, :], idx_raw[:, :], 0, VOCAB - 1, ALU.max, ALU.min).then_inc(idx_done, 1)
            dve.wait_ge(idx_done, 3)
            dve.wait_ge(base_ready, 1)
            nc.vector.tensor_tensor(idx_row[:, :], idx_raw[:, :], idx_base[:, :], ALU.add).then_inc(idx_done, 1)
            dve.wait_ge(idx_done, 4)
            nc.vector.tensor_copy(idx_step[:, 0:HEAD_COLS], idx_row[:, 0:HEAD_COLS]).then_inc(head_staged, 1)
            nc.vector.tensor_copy(idx_step[:, HEAD_COLS:STEP_COLS], idx_row[:, HEAD_COLS:STEP_COLS])\
                .then_inc(rest_staged, 1)
            nc.vector.memset(vecs_st[:, :, :, :, :], 0.0).then_inc(pads_ready, 1)
            nc.vector.memset(feat_t[:, :, KTILES - 1, :], 1.0).then_inc(pads_ready, 1)
            dve.wait_ge(bottom_loaded, 16 * 7)
            bottom(0)
            dve.wait_ge(top_loaded, 16 * 5)
            dve.wait_ge(pads_ready, 2)
            step(0, top=False, do_bottom=True)
            with dve.Fori(1, STEPS - 1) as i:
                step(i, top=True, do_bottom=True)
            step(STEPS - 1, top=True, do_bottom=False)


def kernel(**inputs):
    import concourse.bacc as bacc
    from concourse.bass_utils import run_bass_kernel_spmd as run

    def get(name):
        return np.ascontiguousarray(inputs[name])

    order = top_row_order()
    wt0_rows = np.concatenate([get("L0_rec_Wt0"), get("L0_rec_bt0").reshape(1, T0),
                               np.zeros((1, T0), np.float32)])
    zero, bias = len(wt0_rows) - 1, len(wt0_rows) - 2

    def by_sample(a):
        return a.reshape(2, 2, SLOTS, STEPS, 2, -1)

    arrays = {
        "x": np.ascontiguousarray(by_sample(get("r_dense")).transpose(5, 3, 1, 0, 4, 2)).reshape(DENSE, BATCH),
        "idx": np.ascontiguousarray(by_sample(get("r_sparse_idx")).transpose(0, 4, 2, 3, 5, 1)).reshape(P, -1),
        "emb": get("L0_rec_emb"),
        "wb0": get("L0_rec_Wb0"),
        "bb0": np.ascontiguousarray(get("L0_rec_bb0").reshape(B0 // P, P).T),
        "wb1": get("L0_rec_Wb1"),
        "bb1": np.ascontiguousarray(get("L0_rec_bb1").reshape(B1 // P, P).T),
        "wb2": get("L0_rec_Wb2"),
        "bb2": get("L0_rec_bb2").reshape(DIM, 1),
        "wt0": wt0_rows[np.where(order == -1, zero, np.where(order == -2, bias, order))],
        "wt1": get("L0_rec_Wt1"),
        "bt1": get("L0_rec_bt1"),
        "wt2": get("L0_rec_Wt2").reshape(T1),
        "bt2": get("L0_rec_bt2").reshape(1),
    }
    nc = bacc.Bacc("TRN2", target_bir_lowering=False, num_devices=1)
    args = [nc.dram_tensor("in_" + name, a.shape, mybir.dt.from_np(a.dtype), kind="ExternalInput").ap()
            for name, a in arrays.items()]
    out = nc.dram_tensor("out_0", (BATCH,), F32, kind="ExternalOutput").ap()
    build(nc, *args, out)
    result = run(nc, [{"in_" + name: a for name, a in arrays.items()}], core_ids=[0])
    return result.results[0]["out_0"]
```

```python
from contextlib import ExitStack

import concourse.bass as bass
from concourse import mybir
import numpy as np

ALU = mybir.AluOpType
ACT = mybir.ActivationFunctionType
F32 = mybir.dt.float32
I32 = mybir.dt.int32

P = 128
BATCH = 2048
TABLES = 26
VOCAB = 12500
DIM = 64
DENSE = 13
B0, B1 = 512, 256
T0, T1 = 512, 256
STEP = 2 * P
STEPS = BATCH // STEP
CHUNK = 4 * P
CHUNKS = BATCH // CHUNK
FIRST_CHUNKS = CHUNKS // 2

VECS = TABLES + 1
DSLOT = TABLES
SLOTS = 32
DELTAS = (VECS - 1) // 2
WRAP = VECS + DELTAS
PAIR_TILES = 3
PAIR_ROWS = DELTAS * VECS // PAIR_TILES
D_ROWS = DIM + 1

BOTTOM_LOADS = 7

RUNS = [(t, min(4, TABLES - t)) for t in range(0, TABLES, 4)]
NR = len(RUNS)
ACT_RUNS = (NR + 1) // 2
DVE_RUNS = NR // 2
HEAD = 4
HEAD_COLS = 2 * RUNS[HEAD][0]
STEP_COLS = 2 * TABLES

HALF = 16


def top_row_order():
    order = np.full((PAIR_TILES + 1, P), DIM + DELTAS * VECS + 1, np.int64)
    for delta in range(1, DELTAS + 1):
        for i in range(VECS):
            j = (i + delta) % VECS
            hi, lo = max(i, j), min(i, j)
            tile, row = divmod((delta - 1) * VECS + i, PAIR_ROWS)
            order[tile, row] = DIM + hi * (hi - 1) // 2 + lo
    order[PAIR_TILES, 0:DIM] = np.arange(DIM)
    order[PAIR_TILES, DIM] = DIM + DELTAS * VECS
    return order


def build(nc, x, idx, emb, wb0, bb0, wb1, bb1, wb2, bb2, wt0, wt1, bt1, wt2, bt2, out):
    emb_rows = emb.rearrange("t v d -> (t v) d")

    with ExitStack() as ctx:
        def sb(name, shape, dt=F32):
            return ctx.enter_context(nc.sbuf_tensor(name, shape, dt))

        def ps(name, shape):
            return ctx.enter_context(nc.psum_tensor(name, shape, F32))

        def sem(name):
            return ctx.enter_context(nc.semaphore(name))

        wb0_sb = sb("wb0_sb", [DENSE, B0])
        wb1_sb = sb("wb1_sb", [P, B0 // P, B1])
        wb2_sb = sb("wb2_sb", [P, B1 // P, DIM])
        wt0_sb = sb("wt0_sb", [P, PAIR_TILES + 1, T0])
        wt1_sb = sb("wt1_sb", [P, T0 // P, T1])
        bb0_sb = sb("bb0_sb", [P, B0 // P])
        bb1_sb = sb("bb1_sb", [P, B1 // P])
        bb2_sb = sb("bb2_sb", [DIM, 1])
        bt1_sb = sb("bt1_sb", [1, T1])
        wt2_sb = sb("wt2_sb", [P, T1])
        bt2_sb = sb("bt2_sb", [P, 1])
        ident = sb("ident", [P, P])
        ones = sb("ones", [P, P])
        idx_raw = sb("idx_raw", [P, STEPS * STEP_COLS], I32)
        idx_neg = sb("idx_neg", [P, STEPS * STEP_COLS], I32)
        idx_base = sb("idx_base", [P, STEPS * STEP_COLS], I32)
        idx_row = sb("idx_row", [P, STEPS * STEP_COLS], I32)
        idx_step = sb("idx_step", [P, STEP_COLS], I32)
        x_t = sb("x_t", [DENSE, BATCH])
        hb0 = sb("hb0", [P, B0 // P, CHUNK])
        hb1 = sb("hb1", [P, B1 // P, CHUNK])
        d_all = sb("d_all", [DIM, BATCH])
        d_t = sb("d_t", [D_ROWS, 2, P])
        rows = sb("rows", [P, TABLES, 2 * DIM])
        vecs_st = sb("vecs_st", [P, P, SLOTS])
        vecs_mv = sb("vecs_mv", [P, P, 2, VECS])
        gram_s = [sb(f"gram_s{u}", [P, WRAP * SLOTS]) for u in range(2)]
        feat = sb("feat", [P, 2, DELTAS * VECS])
        feat_t = sb("feat_t", [PAIR_ROWS, 2, PAIR_TILES, P])
        ht0_t = sb("ht0_t", [P, T0 // P, P])
        ht1_w = sb("ht1_w", [P, T1])
        logits = sb("logits", [P, 2 * STEPS])
        probs = sb("probs", [P, 2 * STEPS])

        ps_turn = [ps(f"ps_turn{b}", [P, 4, P]) for b in range(2)]
        ps_gram = ps("ps_gram", [P, 2, 512])
        ps_feat = [ps(f"ps_feat{u}", [P, 4, P]) for u in range(2)]
        ps_t0 = ps("ps_t0", [P, 512])
        ps_t1 = ps("ps_t1", [P, 512])

        idx_loaded = sem("idx_loaded")
        bottom_loaded = sem("bottom_loaded")
        top_loaded = sem("top_loaded")
        base_ready = sem("base_ready")
        filled = sem("filled")
        table_ready = sem("table_ready")
        ident_ready = sem("ident_ready")
        pads_ready = sem("pads_ready")
        idx_done = sem("idx_done")
        head_staged = sem("head_staged")
        rest_staged = sem("rest_staged")
        gathers_begun = sem("gathers_begun")
        rows_landed = [sem(f"rows_landed{r}") for r in range(NR)]
        rows_landed_last = [[sem(f"rows_landed_last{h}_{r}") for r in range(NR)] for h in range(2)]
        rows_turned = sem("rows_turned")
        b0_summed = sem("b0_summed")
        b0_act = sem("b0_act")
        b0_dve = sem("b0_dve")
        b1_summed = sem("b1_summed")
        b1_act = sem("b1_act")
        b1_dve = sem("b1_dve")
        b2_summed = sem("b2_summed")
        d_ready = sem("d_ready")
        d_placed = sem("d_placed")
        d_copied = sem("d_copied")
        vecs_act = sem("vecs_act")
        vecs_dve = sem("vecs_dve")
        gram_summed = sem("gram_summed")
        gram_turned = sem("gram_turned")
        feat_packed = sem("feat_packed")
        feat_turned = sem("feat_turned")
        feat_act = sem("feat_act")
        t0_summed = sem("t0_summed")
        t0_act = sem("t0_act")
        t0_dve = sem("t0_dve")
        t1_summed = sem("t1_summed")
        logit_ready = sem("logit_ready")
        probs_ready = sem("probs_ready")
        out_stored = sem("out_stored")

        ps_b0 = [ps_gram[:, 0, :], ps_gram[:, 1, :], ps_feat[0][:, :, :].rearrange("p a c -> p (a c)"),
                 ps_feat[1][:, :, :].rearrange("p a c -> p (a c)")]

        ps_b2 = ps_turn[0][0:DIM, :, :].rearrange("p a c -> p (a c)")

        def top_0_blocks(u, side):
            if side == 0:
                return ps_t0[:, 0:2 * P].rearrange("p (m c) -> p m c", m=2)
            return ps_feat[u][:, 0:2, :]

        def turned_rows(r):
            first, n = RUNS[r]
            bank = ps_turn[r % 2]
            yield vecs_st[:, :, first:first + n].rearrange("p c t -> p t c"), bank[:, 0:n, :]
            for h in range(2):
                part = slice(DIM * h, DIM * (h + 1))
                yield vecs_mv[part, :, h, first:first + n].rearrange("p c t -> p t c"), bank[part, 0:n, :]

        def unit_products(n):
            return ps_gram[:, :, 0:HALF * VECS].rearrange("p b (c v) -> p v b c", v=VECS)[:, 0:n]

        def turned_half(h, r):
            first, n = RUNS[r]
            part = slice(DIM * h, DIM * (h + 1))
            return (vecs_st[part, :, first:first + n].rearrange("p c t -> p t c"),
                    ps_turn[(h * NR + r) % 2][part, 0:n, :])

        block = ctx.enter_context(nc.Block())

        @block.sync
        def _(sp):
            sp.dma_start(idx_raw[:, :], idx).then_inc(idx_loaded, 16)
            sp.dma_start(wb0_sb[:, :], wb0).then_inc(bottom_loaded, 16)
            sp.dma_start(wb1_sb[:, :, :], wb1.rearrange("(k p) n -> p k n", p=P)).then_inc(bottom_loaded, 16)
            sp.dma_start(wb2_sb[:, :, :], wb2.rearrange("(k p) n -> p k n", p=P)).then_inc(bottom_loaded, 16)
            sp.dma_start(wt0_sb[:, :, :], wt0.rearrange("k p n -> p k n")).then_inc(top_loaded, 16)
            sp.dma_start(wt1_sb[:, :, :], wt1.rearrange("(k p) n -> p k n", p=P)).then_inc(top_loaded, 16)
            sp.wait_ge(probs_ready, 1)
            sp.dma_start(out.rearrange("(p n) -> p n", p=P), probs[:, :]).then_inc(out_stored, 16)
            sp.wait_ge(out_stored, 16)

        @block.gpsimd
        def _(pool):
            nc.gpsimd.iota(idx_base[:, :], [[0, STEPS], [VOCAB, TABLES], [0, 2]], base=0,
                           channel_multiplier=0).then_inc(base_ready, 1)
            pool.wait_ge(filled, 1)
            nc.gpsimd.affine_select(out=ident[:, :], in_=ones[:, :], pattern=[[-1, P]], compare_op=ALU.is_equal,
                                    fill=0.0, base=0, channel_multiplier=1).then_inc(ident_ready, 1)
            pool.sem_inc(rows_turned, NR)
            parts = ((head_staged, 0, HEAD // 2), (head_staged, HEAD // 2, HEAD), (rest_staged, HEAD, NR))

            def begin(i, staged, hi):
                pool.wait_ge(staged, i + 1)
                pool.wait_ge(rows_turned, i * NR + hi)
                pool.sem_inc(gathers_begun, 1)

            def gather(t, h, landed):
                c = 2 * t + h
                nc.gpsimd.indirect_dma_start(
                    rows[:, t, h * DIM:(h + 1) * DIM], None, emb_rows,
                    bass.IndirectOffsetOnAxis(idx_step[:, c:c + 1], 0)).then_inc(landed, 16)

            with pool.Fori(0, STEPS - 1) as i:
                for staged, lo, hi in parts:
                    begin(i, staged, hi)
                    for r in range(lo, hi):
                        first, n = RUNS[r]
                        for t in range(first, first + n):
                            for h in range(2):
                                gather(t, h, rows_landed[r])
            for h in range(2):
                for staged, lo, hi in parts:
                    if h == 0:
                        begin(STEPS - 1, staged, hi)
                    for r in range(lo, hi):
                        first, n = RUNS[r]
                        for t in range(first, first + n):
                            gather(t, h, rows_landed_last[h][r])

        @block.tensor
        def _(pe):
            def bottom_0(c):
                for m in range(B0 // P):
                    nc.tensor.matmul(ps_b0[m], wb0_sb[:, m * P:(m + 1) * P], x_t[:, bass.ds(c * CHUNK, CHUNK)],
                                     start=True, stop=True).then_inc(b0_summed, 1)

            def bottom_12(c, last=False):
                pe.wait_ge(b0_act, c + 1)
                pe.wait_ge(b0_dve, c + 1)
                for m in range(B1 // P):
                    for k in range(B0 // P):
                        summed = nc.tensor.matmul((ps_t0, ps_t1)[m][:, :], wb1_sb[:, k, m * P:(m + 1) * P],
                                                  hb0[:, k, :], start=(k == 0), stop=(k == B0 // P - 1))
                    summed.then_inc(b1_summed, 1)
                if not last:
                    bottom_0(c + 1)
                pe.wait_ge(b1_act, c + 1)
                pe.wait_ge(b1_dve, c + 1)
                for k in range(B1 // P):
                    summed = nc.tensor.matmul(ps_b2, wb2_sb[:, k, :], hb1[:, k, :],
                                              start=(k == 0), stop=(k == B1 // P - 1))
                summed.then_inc(b2_summed, 1)

            def turn(i, r):
                first, n = RUNS[r]
                pe.wait_ge(rows_landed[r], (i + 1) * (32 * n))
                if r >= 2 and r % 2 == 0:
                    pe.wait_ge(vecs_act, i * ACT_RUNS + r // 2)
                if r >= 2 and r % 2 == 1:
                    pe.wait_ge(vecs_dve, i * DVE_RUNS + r // 2)
                for j in range(n):
                    turned = nc.tensor.transpose(ps_turn[r % 2][:, j, :], rows[:, first + j, :], ident[:, :])
                turned.then_inc(rows_turned, 1)

            def turn_last(h, r):
                first, n = RUNS[r]
                k = h * NR + r
                pe.wait_ge(rows_landed_last[h][r], 16 * n)
                if k >= 2 and k % 2 == 0:
                    pe.wait_ge(vecs_act, (STEPS - 1) * ACT_RUNS + k // 2)
                if k >= 2 and k % 2 == 1:
                    pe.wait_ge(vecs_dve, (STEPS - 1) * DVE_RUNS + k // 2)
                cols = DIM * (h + 1)
                for j in range(n):
                    turned = nc.tensor.transpose(ps_turn[k % 2][0:cols, j, :], rows[:, first + j, 0:cols], ident[:, :])
                turned.then_inc(rows_turned, 1)

            def gram(i, u):
                if u == 0:
                    pe.wait_ge(vecs_act, (i + 1) * ACT_RUNS)
                    pe.wait_ge(vecs_dve, (i + 1) * DVE_RUNS)
                    pe.wait_ge(d_placed, i + 1)
                else:
                    pe.wait_ge(gram_turned, i * 4 + 2)
                for b in range(2):
                    for g in range(HALF // 2):
                        for v in range(4):
                            c = 64 * u + 16 * v + b * (HALF // 2) + g
                            summed = nc.tensor.matmul(
                                ps_gram[32 * v:32 * v + 32, b, g * 2 * VECS:(g + 1) * 2 * VECS],
                                vecs_st[:, c, :], vecs_mv[:, c, :, :].rearrange("p h t -> p (h t)"),
                                start=True, stop=True)
                summed.then_inc(gram_summed, 1)

            def gram_last(h):
                i = STEPS - 1
                pe.wait_ge(vecs_act, i * ACT_RUNS + (NR * (h + 1) + 1) // 2)
                pe.wait_ge(vecs_dve, i * DVE_RUNS + NR * (h + 1) // 2)
                if h == 0:
                    pe.wait_ge(d_placed, STEPS)
                else:
                    pe.wait_ge(gram_turned, i * 4 + 2)
                part = slice(DIM * h, DIM * (h + 1))
                for u in range(2):
                    for g in range(HALF):
                        for v in range(4):
                            c = 64 * u + 16 * v + g
                            summed = nc.tensor.matmul(
                                ps_gram[32 * v:32 * v + 32, u, g * VECS:(g + 1) * VECS],
                                vecs_st[part, c, :], vecs_st[part, c, 0:VECS],
                                start=True, stop=True, tile_position=(DIM * h, 32 * v))
                summed.then_inc(gram_summed, 1)

            def turn_feat(i, u):
                pe.wait_ge(feat_packed, i * 2 + u + 1)
                for k in range(PAIR_TILES):
                    turned = nc.tensor.transpose(ps_feat[u][0:PAIR_ROWS, k, :],
                                                 feat[:, u, k * PAIR_ROWS:(k + 1) * PAIR_ROWS], ident[:, :])
                turned.then_inc(feat_turned, 1)

            def top_0_d(i, u, m):
                if m == 0 and u == 0:
                    pe.wait_ge(d_copied, i + 1)
                if m == 0 and u == 1:
                    pe.wait_ge(t0_act, i * 2 + 1)
                nc.tensor.matmul(top_0_blocks(u, m // 2)[:, m % 2, :], wt0_sb[0:D_ROWS, PAIR_TILES, m * P:(m + 1) * P],
                                 d_t[:, u, :], start=True, stop=False)

            def top_0_pairs(i, u, m):
                for k in range(PAIR_TILES):
                    summed = nc.tensor.matmul(top_0_blocks(u, m // 2)[:, m % 2, :],
                                              wt0_sb[0:PAIR_ROWS, k, m * P:(m + 1) * P],
                                              feat_t[:, u, k, :], start=False, stop=(k == PAIR_TILES - 1))
                if m % 2 == 1:
                    summed.then_inc(t0_summed, 1)

            def top_0(i, u, blocks=range(T0 // P), begun=False):
                for m in blocks:
                    if m > 0 or not begun:
                        top_0_d(i, u, m)
                    if m == 0:
                        pe.wait_ge(feat_act, i * 2 + u + 1)
                    top_0_pairs(i, u, m)

            def top_1_bias(i, u):
                if u == 1:
                    pe.wait_ge(logit_ready, i * 2 + 1)
                nc.tensor.matmul(ps_t1[:, 0:T1], ones[0:1, :], bt1_sb[:, :], start=True, stop=False)

            def top_1_sum(i, u):
                for k in range(T0 // P):
                    if k == 0:
                        pe.wait_ge(t0_act, i * 2 + u + 1)
                    if k == 2:
                        pe.wait_ge(t0_dve, i * 2 + u + 1)
                    summed = nc.tensor.matmul(ps_t1[:, 0:T1], ht0_t[:, k, :], wt1_sb[:, k, :],
                                              start=False, stop=(k == T0 // P - 1))
                summed.then_inc(t1_summed, 1)

            def top_1(i, u):
                top_1_bias(i, u)
                top_1_sum(i, u)

            def first_step():
                for c in range(FIRST_CHUNKS, CHUNKS):
                    pe.wait_ge(d_ready, c)
                    turn(0, 2 * (c - FIRST_CHUNKS))
                    turn(0, 2 * (c - FIRST_CHUNKS) + 1)
                    bottom_12(c, last=(c == CHUNKS - 1))
                pe.wait_ge(d_ready, CHUNKS)
                for r in range(2 * (CHUNKS - FIRST_CHUNKS), NR):
                    turn(0, r)
                gram(0, 0)
                gram(0, 1)
                turn_feat(0, 0)
                turn_feat(0, 1)

            def land(i, turn_run):
                turn_run(0)
                top_0(i - 1, 0)
                turn_run(1)
                turn_run(2)
                top_1(i - 1, 0)
                top_0(i - 1, 1)
                turn_run(3)
                turn_run(4)
                top_1(i - 1, 1)
                turn_run(5)
                turn_run(6)

            def step(i):
                land(i, lambda r: turn(i, r))
                gram(i, 0)
                gram(i, 1)
                turn_feat(i, 0)
                turn_feat(i, 1)

            def last_step():
                i = STEPS - 1
                land(i, lambda r: turn_last(0, r))
                gram_last(0)
                turn_last(1, 0)
                turn_feat(i, 0)
                for r in range(1, NR - 3):
                    turn_last(1, r)
                top_0(i, 0, blocks=range(0, 2))
                turn_last(1, NR - 3)
                top_0(i, 0, blocks=range(2, 4))
                top_1_bias(i, 0)
                turn_last(1, NR - 2)
                top_1_sum(i, 0)
                turn_last(1, NR - 1)
                gram_last(1)
                top_0_d(i, 1, 0)
                top_1_bias(i, 1)
                turn_feat(i, 1)
                top_0(i, 1, begun=True)
                top_1_sum(i, 1)

            pe.wait_ge(bottom_loaded, 16 * BOTTOM_LOADS)
            bottom_0(0)
            with pe.Fori(0, FIRST_CHUNKS) as c:
                bottom_12(c)
            pe.wait_ge(ident_ready, 1)
            first_step()
            pe.wait_ge(top_loaded, 16 * 5)
            with pe.Fori(1, STEPS - 1) as i:
                step(i)
            last_step()

        @block.scalar
        def _(act):
            def bottom_0(c):
                for m in range(2):
                    act.wait_ge(b0_summed, c * 4 + m + 1)
                    moved = nc.scalar.activation(hb0[:, m, :], ps_b0[m], ACT.Relu, bias=bb0_sb[:, m:m + 1])
                moved.then_inc(b0_act, 1)

            def bottom_12(c, last=False):
                act.wait_ge(b1_summed, c * 2 + 1)
                nc.scalar.activation(hb1[:, 0, :], ps_t0[:, :], ACT.Relu, bias=bb1_sb[:, 0:1]).then_inc(b1_act, 1)
                if not last:
                    bottom_0(c + 1)
                act.wait_ge(b2_summed, c + 1)
                nc.scalar.activation(d_all[:, bass.ds(c * CHUNK, CHUNK)], ps_b2, ACT.Relu,
                                     bias=bb2_sb[:, 0:1]).then_inc(d_ready, 1)

            def place_d(i, last=False):
                for h in range(2):
                    d = d_all[:, bass.ds(i * STEP + h * P, P)]
                    part = slice(DIM * h, DIM * (h + 1))
                    placed = nc.scalar.activation(vecs_st[part, :, DSLOT], d, ACT.Copy)
                    if not last:
                        placed = nc.scalar.activation(vecs_mv[part, :, h, DSLOT], d, ACT.Copy)
                placed.then_inc(d_placed, 1)

            def spread(i, r):
                act.wait_ge(rows_turned, i * NR + r + 1 + NR)
                for to, source in turned_rows(r):
                    moved = nc.scalar.activation(to, source, ACT.Copy)
                moved.then_inc(vecs_act, 1)

            def spread_last(h, r):
                act.wait_ge(rows_turned, (STEPS + h) * NR + r + 1)
                nc.scalar.activation(*turned_half(h, r), ACT.Copy).then_inc(vecs_act, 1)

            def copy_d(i, last=False):
                d = d_all[:, bass.ds(i * STEP, STEP)]
                if last:
                    for h in range(2):
                        copied = nc.scalar.activation(
                            d_t[0:DIM, h, :].rearrange("d (v u g) -> d v u g", v=4, u=2),
                            d[:, h * P:(h + 1) * P].rearrange("d (u v g) -> d v u g", u=2, v=4), ACT.Copy)
                else:
                    copied = nc.scalar.activation(d_t[0:DIM, :, :].rearrange("d u (c h) -> d u c h", h=2),
                                                  d.rearrange("d (h u c) -> d u c h", h=2, u=2), ACT.Copy)
                copied.then_inc(d_copied, 1)

            def pack(i, u):
                act.wait_ge(gram_turned, i * 4 + 2 * u + 2)
                nc.scalar.activation(feat[:, u, :].rearrange("p (e i) -> p e i", e=DELTAS),
                                     bass.AP(gram_s[u], SLOTS, [[WRAP * SLOTS, P], [SLOTS, DELTAS], [SLOTS + 1, VECS]]),
                                     ACT.Copy).then_inc(feat_packed, 1)

            def move_feat(i, u):
                act.wait_ge(feat_turned, i * 2 + u + 1)
                nc.scalar.activation(feat_t[:, u, :, :], ps_feat[u][0:PAIR_ROWS, 0:PAIR_TILES, :],
                                     ACT.Copy).then_inc(feat_act, 1)

            def relu_top(i, u):
                act.wait_ge(t0_summed, i * 4 + 2 * u + 1)
                nc.scalar.activation(ht0_t[:, 0:2, :], top_0_blocks(u, 0), ACT.Relu).then_inc(t0_act, 1)

            def land(i, spread_run, last=False):
                spread_run(0)
                place_d(i, last)
                relu_top(i - 1, 0)
                spread_run(2)
                relu_top(i - 1, 1)
                spread_run(4)
                copy_d(i, last)
                spread_run(6)

            def pair_rows(i):
                pack(i, 0)
                move_feat(i, 0)
                pack(i, 1)
                move_feat(i, 1)

            def first_step():
                act.wait_ge(d_ready, FIRST_CHUNKS)
                spread(0, 0)
                place_d(0)
                copy_d(0)
                for c in range(FIRST_CHUNKS, CHUNKS):
                    bottom_12(c, last=(c == CHUNKS - 1))
                    spread(0, 2 * (c - FIRST_CHUNKS) + 2)
                spread(0, 6)
                pair_rows(0)

            def step(i):
                land(i, lambda r: spread(i, r))
                pair_rows(i)

            def last_step():
                i = STEPS - 1
                land(i, lambda r: spread_last(0, r), last=True)
                pack(i, 0)
                move_feat(i, 0)
                spread_last(1, 1)
                spread_last(1, 3)
                relu_top(i, 0)
                spread_last(1, 5)
                pack(i, 1)
                move_feat(i, 1)
                relu_top(i, 1)

            act.dma_start(x_t[:, :], x).then_inc(bottom_loaded, 16)
            act.dma_start(bb0_sb[:, :], bb0).then_inc(bottom_loaded, 16)
            act.dma_start(bb1_sb[:, :], bb1).then_inc(bottom_loaded, 16)
            act.dma_start(bb2_sb[:, :], bb2).then_inc(bottom_loaded, 16)
            act.dma_start(bt1_sb[:, :], bt1).then_inc(top_loaded, 16)
            act.dma_start(wt2_sb[:, :], wt2.partition_broadcast(P)).then_inc(top_loaded, 16)
            act.dma_start(bt2_sb[:, :], bt2.partition_broadcast(P)).then_inc(top_loaded, 16)
            act.wait_ge(filled, 1)
            nc.scalar.activation(probs[:, 0:1], ones[:, 0:1], ACT.Sigmoid).then_inc(table_ready, 1)
            act.wait_ge(bottom_loaded, 16 * BOTTOM_LOADS)
            act.wait_ge(pads_ready, 3)
            bottom_0(0)
            with act.Fori(0, FIRST_CHUNKS) as c:
                bottom_12(c)
            first_step()
            act.wait_ge(d_ready, CHUNKS)
            with act.Fori(1, STEPS - 1) as i:
                step(i)
            last_step()
            act.wait_ge(top_loaded, 16 * 5)
            act.wait_ge(logit_ready, 2 * STEPS)
            act.wait_ge(table_ready, 1)
            nc.scalar.activation(probs[:, :], logits[:, :], ACT.Sigmoid, bias=bt2_sb[:, 0:1]).then_inc(probs_ready, 1)

        @block.vector
        def _(dve):
            def stage(i, staged, lo, hi, runs):
                for r in runs:
                    dve.wait_ge(rows_landed[r], (i + 1) * (32 * RUNS[r][1]))
                nc.vector.tensor_copy(idx_step[:, lo:hi], idx_row[:, bass.ds(i * STEP_COLS + (STEP_COLS + lo), hi - lo)])\
                    .then_inc(staged, 1)

            def bottom_0(c):
                for m in range(2, 4):
                    dve.wait_ge(b0_summed, c * 4 + m + 1)
                    moved = nc.vector.tensor_scalar(hb0[:, m, :], ps_b0[m], bb0_sb[:, m:m + 1], 0.0, ALU.add, ALU.max)
                moved.then_inc(b0_dve, 1)

            def bottom_12(c, last=False):
                dve.wait_ge(b1_summed, c * 2 + 2)
                nc.vector.tensor_scalar(hb1[:, 1, :], ps_t1[:, :], bb1_sb[:, 1:2], 0.0,
                                        ALU.add, ALU.max).then_inc(b1_dve, 1)
                if not last:
                    bottom_0(c + 1)

            def spread(i, r):
                dve.wait_ge(rows_turned, i * NR + r + 1 + NR)
                for to, source in turned_rows(r):
                    moved = nc.vector.tensor_copy(to, source)
                moved.then_inc(vecs_dve, 1)

            def spread_last(h, r):
                dve.wait_ge(rows_turned, (STEPS + h) * NR + r + 1)
                nc.vector.tensor_copy(*turned_half(h, r)).then_inc(vecs_dve, 1)

            def turn_gram(i, u):
                dve.wait_ge(gram_summed, i * 2 + u + 1)
                nc.vector.transpose(gram_s[u][:, 0:VECS * SLOTS], unit_products(VECS)).then_inc(gram_turned, 1)
                nc.vector.transpose(gram_s[u][:, VECS * SLOTS:WRAP * SLOTS], unit_products(DELTAS))\
                    .then_inc(gram_turned, 1)

            def relu_top(i, u):
                dve.wait_ge(t0_summed, i * 4 + 2 * u + 2)
                nc.vector.tensor_scalar(ht0_t[:, 2:4, :], top_0_blocks(u, 1), 0.0, None, ALU.max).then_inc(t0_dve, 1)

            def logit(i, u):
                dve.wait_ge(t1_summed, i * 2 + u + 1)
                nc.vector.scalar_tensor_tensor(out=ht1_w[:, :], in0=ps_t1[:, 0:T1], scalar=0.0, in1=wt2_sb[:, :],
                                               op0=ALU.max, op1=ALU.mult,
                                               accum_out=logits[:, bass.ds(i * 2 + u, 1)]).then_inc(logit_ready, 1)

            def stage_head(i):
                stage(i, head_staged, 0, HEAD_COLS, range(HEAD))

            def land(i, spread_run, head=None):
                spread_run(1)
                relu_top(i - 1, 0)
                logit(i - 1, 0)
                spread_run(3)
                if head:
                    head()
                relu_top(i - 1, 1)
                logit(i - 1, 1)
                spread_run(5)

            def products(i):
                turn_gram(i, 0)
                stage(i, rest_staged, HEAD_COLS, STEP_COLS, range(HEAD, NR))
                turn_gram(i, 1)

            def first_step():
                spread(0, 1)
                stage_head(0)
                for c in range(FIRST_CHUNKS, CHUNKS):
                    bottom_12(c, last=(c == CHUNKS - 1))
                    spread(0, 2 * (c - FIRST_CHUNKS) + 3)
                products(0)

            def step(i):
                land(i, lambda r: spread(i, r), lambda: stage_head(i))
                products(i)

            def last_step():
                i = STEPS - 1
                land(i, lambda r: spread_last(0, r))
                turn_gram(i, 0)
                spread_last(1, 0)
                spread_last(1, 2)
                spread_last(1, 4)
                relu_top(i, 0)
                spread_last(1, 6)
                logit(i, 0)
                turn_gram(i, 1)
                relu_top(i, 1)
                logit(i, 1)

            nc.vector.memset(ones[:, :], 1.0).then_inc(filled, 1)
            dve.wait_ge(idx_loaded, 16)
            dve.wait_ge(base_ready, 1)
            for n, (lo, hi) in enumerate(((0, STEP_COLS), (STEP_COLS, STEPS * STEP_COLS))):
                raw = idx_raw[:, lo:hi]
                nc.vector.tensor_scalar(idx_neg[:, lo:hi], raw, 0, VOCAB, ALU.is_lt, ALU.mult).then_inc(idx_done, 1)
                dve.wait_ge(idx_done, n * 4 + 1)
                nc.vector.tensor_tensor(raw, raw, idx_neg[:, lo:hi], ALU.add).then_inc(idx_done, 1)
                dve.wait_ge(idx_done, n * 4 + 2)
                nc.vector.tensor_scalar(raw, raw, 0, VOCAB - 1, ALU.max, ALU.min).then_inc(idx_done, 1)
                dve.wait_ge(idx_done, n * 4 + 3)
                if n == 0:
                    nc.vector.tensor_tensor(idx_step[:, 0:HEAD_COLS], raw[:, 0:HEAD_COLS], idx_base[:, 0:HEAD_COLS],
                                            ALU.add).then_inc(head_staged, 1)
                    nc.vector.tensor_tensor(idx_step[:, HEAD_COLS:], raw[:, HEAD_COLS:], idx_base[:, HEAD_COLS:hi],
                                            ALU.add).then_inc(rest_staged, 1)
                nc.vector.tensor_tensor(idx_row[:, lo:hi], raw, idx_base[:, lo:hi], ALU.add).then_inc(idx_done, 1)
            nc.vector.memset(vecs_mv[:, :, :, :], 0.0).then_inc(pads_ready, 1)
            nc.vector.memset(vecs_st[:, :, VECS:SLOTS], 0.0).then_inc(pads_ready, 1)
            nc.vector.memset(d_t[DIM:D_ROWS, :, :], 1.0).then_inc(pads_ready, 1)
            dve.wait_ge(bottom_loaded, 16 * BOTTOM_LOADS)
            bottom_0(0)
            with dve.Fori(0, FIRST_CHUNKS) as c:
                bottom_12(c)
            dve.wait_ge(top_loaded, 16 * 5)
            dve.wait_ge(pads_ready, 3)
            first_step()
            with dve.Fori(1, STEPS - 1) as i:
                step(i)
            last_step()


def kernel(**inputs):
    import concourse.bacc as bacc
    from concourse.bass_utils import run_bass_kernel_spmd as run

    def get(name):
        return np.ascontiguousarray(inputs[name])

    wt0_rows = np.concatenate([get("L0_rec_Wt0"), get("L0_rec_bt0").reshape(1, T0),
                               np.zeros((1, T0), np.float32)])

    def by_step(a, axes, last_axes):
        most = a.reshape(4, 16, 2, STEPS, 2, -1).transpose(axes)
        last = a.reshape(4, 2, 16, STEPS, 2, -1).transpose(last_axes)
        at = axes.index(3)
        return np.concatenate([most.take(range(STEPS - 1), at), last.take([STEPS - 1], at)], at)

    arrays = {
        "x": by_step(get("r_dense"), (5, 3, 2, 4, 0, 1), (5, 3, 4, 1, 0, 2)).reshape(DENSE, BATCH),
        "idx": by_step(get("r_sparse_idx"), (4, 0, 1, 3, 5, 2), (1, 0, 2, 3, 5, 4)).reshape(P, STEPS * STEP_COLS),
        "emb": get("L0_rec_emb"),
        "wb0": get("L0_rec_Wb0"),
        "bb0": np.ascontiguousarray(get("L0_rec_bb0").reshape(B0 // P, P).T),
        "wb1": get("L0_rec_Wb1"),
        "bb1": np.ascontiguousarray(get("L0_rec_bb1").reshape(B1 // P, P).T),
        "wb2": get("L0_rec_Wb2"),
        "bb2": get("L0_rec_bb2").reshape(DIM, 1),
        "wt0": wt0_rows[top_row_order()],
        "wt1": get("L0_rec_Wt1"),
        "bt1": get("L0_rec_bt1").reshape(1, T1),
        "wt2": get("L0_rec_Wt2").reshape(T1),
        "bt2": get("L0_rec_bt2").reshape(1),
    }
    nc = bacc.Bacc("TRN2", target_bir_lowering=False, num_devices=1)
    args = [nc.dram_tensor("in_" + name, a.shape, mybir.dt.from_np(a.dtype), kind="ExternalInput").ap()
            for name, a in arrays.items()]
    out = nc.dram_tensor("out_0", (BATCH,), F32, kind="ExternalOutput").ap()
    build(nc, *args, out)
    result = run(nc, [{"in_" + name: a for name, a in arrays.items()}], core_ids=[0])
    return result.results[0]["out_0"]
```
